# Optimizing a Trainium2 kernel written in Bass

```python
import numpy as np
import jax
import jax.numpy as jnp

def _softmax(x, axis=-1):
    return jax.nn.softmax(x, axis=axis)

def _gelu(x):
    return jax.nn.gelu(x, approximate=True)

def _silu(x):
    return jax.nn.silu(x)

def _sigmoid(x):
    return jax.nn.sigmoid(x)

def _layernorm(x, axis=-1, eps=1e-05):
    m = jnp.mean(x, axis=axis, keepdims=True)
    v = jnp.var(x, axis=axis, keepdims=True)
    return (x - m) / jnp.sqrt(v + eps)

def _scatter_add(tgt, idx, src, axis=0):
    return tgt.at[idx].add(src)

def _segment_sum(src, seg, n):
    return jax.ops.segment_sum(src, seg, n)
kernel_name = 'mk_macaron_d1_jaxref_r8_874586'

def setup_inputs(seed: int=0):
    np.random.seed(seed)
    _w = jnp.asarray

    def _L0_attn_setup():
        import jax, jax.numpy as jnp
        import numpy as np
        B, T, C = (64, 32, 128)
        N_HEAD, HEAD_SIZE, KV_RANK = (16, 64, 128)
        BLOCK_SIZE = 32
        key = jax.random.key(seed)
        ks = jax.random.split(key, 5)
        HD = N_HEAD * HEAD_SIZE

        def init(k, shape):
            fan_in = shape[0]
            bound = 1.0 / np.sqrt(fan_in)
            return jax.random.uniform(k, shape, jnp.float32, -bound, bound)
        return {'x': jax.random.normal(ks[0], (B, T, C), jnp.float32), 'w_kv_down': init(ks[1], (C, KV_RANK)), 'w_kv_up': init(ks[2], (KV_RANK, 2 * HD)), 'w_q': init(ks[3], (C, HD)), 'w_out': init(ks[4], (HD, C))}
    _L0_attn_in = _L0_attn_setup()

    def _L0_ffn_setup():
        import jax, jax.numpy as jnp
        import numpy as np
        D_MODEL = 128
        HIDDEN = 512
        NUM_EXPERTS = 8
        TOP_K = 2
        NUM_SHARED = 2

        def _gelu(x):
            return jax.nn.gelu(x, approximate=False)
        key = jax.random.key(seed)
        ks = jax.random.split(key, 12)
        s = 0.02
        return {'x': jax.random.normal(ks[0], (2, 256, D_MODEL), dtype=jnp.float32), 'rW': jax.random.normal(ks[1], (D_MODEL, NUM_EXPERTS), dtype=jnp.float32) * s, 'rb': jnp.zeros((NUM_EXPERTS,), dtype=jnp.float32), 'W1': jax.random.normal(ks[2], (NUM_EXPERTS, D_MODEL, HIDDEN), dtype=jnp.float32) * s, 'b1': jnp.zeros((NUM_EXPERTS, HIDDEN), dtype=jnp.float32), 'W2': jax.random.normal(ks[3], (NUM_EXPERTS, HIDDEN, D_MODEL), dtype=jnp.float32) * s, 'b2': jnp.zeros((NUM_EXPERTS, D_MODEL), dtype=jnp.float32), 'sW1': jax.random.normal(ks[4], (NUM_SHARED, D_MODEL, HIDDEN), dtype=jnp.float32) * s, 'sb1': jnp.zeros((NUM_SHARED, HIDDEN), dtype=jnp.float32), 'sW2': jax.random.normal(ks[5], (NUM_SHARED, HIDDEN, D_MODEL), dtype=jnp.float32) * s, 'sb2': jnp.zeros((NUM_SHARED, D_MODEL), dtype=jnp.float32)}
    _L0_ffn_in = _L0_ffn_setup()
    _d = {'L0_attn_x': _L0_attn_in['x'], 'L0_attn_w_kv_down': _L0_attn_in['w_kv_down'], 'L0_attn_w_kv_up': _L0_attn_in['w_kv_up'], 'L0_attn_w_q': _L0_attn_in['w_q'], 'L0_attn_w_out': _L0_attn_in['w_out'], 'L0_ffn_rW': _L0_ffn_in['rW'], 'L0_ffn_rb': _L0_ffn_in['rb'], 'L0_ffn_W1': _L0_ffn_in['W1'], 'L0_ffn_b1': _L0_ffn_in['b1'], 'L0_ffn_W2': _L0_ffn_in['W2'], 'L0_ffn_b2': _L0_ffn_in['b2'], 'L0_ffn_sW1': _L0_ffn_in['sW1'], 'L0_ffn_sb1': _L0_ffn_in['sb1'], 'L0_ffn_sW2': _L0_ffn_in['sW2'], 'L0_ffn_sb2': _L0_ffn_in['sb2']}
    _x0 = _d['L0_attn_x']
    _d['L0_attn_x'] = jax.random.normal(jax.random.fold_in(jax.random.key(seed), 1), (1, 2048, 128), dtype=_x0.dtype)
    del _x0
    return _d

def reference(L0_attn_x, L0_attn_w_kv_down, L0_attn_w_kv_up, L0_attn_w_q, L0_attn_w_out, L0_ffn_rW, L0_ffn_rb, L0_ffn_W1, L0_ffn_b1, L0_ffn_W2, L0_ffn_b2, L0_ffn_sW1, L0_ffn_sb1, L0_ffn_sW2, L0_ffn_sb2):

    def _L0_attn_ref(x, w_kv_down, w_kv_up, w_q, w_out):
        import jax, jax.numpy as jnp
        import numpy as np
        B, T, C = (64, 32, 128)
        N_HEAD, HEAD_SIZE, KV_RANK = (16, 64, 128)
        BLOCK_SIZE = 32
        Bx, Tx, Cx = x.shape
        HD = N_HEAD * HEAD_SIZE
        latent_kv = x @ w_kv_down
        kv = latent_kv @ w_kv_up
        k, v = (kv[..., :HD], kv[..., HD:])
        k = k.reshape(Bx, Tx, N_HEAD, HEAD_SIZE)
        v = v.reshape(Bx, Tx, N_HEAD, HEAD_SIZE)
        q = (x @ w_q).reshape(Bx, Tx, N_HEAD, HEAD_SIZE)
        scale = HEAD_SIZE ** (-0.5)
        att = jnp.einsum('bqhd,bkhd->bhqk', q, k) * scale
        causal = jnp.tril(jnp.ones((Tx, Tx), dtype=bool))
        att = jnp.where(causal, att, -jnp.inf)
        att = jax.nn.softmax(att, axis=-1)
        y = jnp.einsum('bhqk,bkhd->bqhd', att, v)
        y = y.reshape(Bx, Tx, HD)
        return y @ w_out

    def _L0_ffn_ref(x, rW, rb, W1, b1, W2, b2, sW1, sb1, sW2, sb2):
        import jax, jax.numpy as jnp
        import numpy as np
        D_MODEL = 128
        HIDDEN = 512
        NUM_EXPERTS = 8
        TOP_K = 2
        NUM_SHARED = 2

        def _gelu(x):
            return jax.nn.gelu(x, approximate=False)
        B, L, D = x.shape
        xf = x.reshape(-1, D)
        sh = _gelu(jnp.einsum('td,sdh->sth', xf, sW1) + sb1[:, None, :])
        shared = jnp.einsum('sth,shd->std', sh, sW2) + sb2[:, None, :]
        shared = shared.mean(axis=0)
        gates = xf @ rW + rb
        topk_vals, topk_idx = jax.lax.top_k(gates, TOP_K)
        topk_probs = jax.nn.softmax(topk_vals, axis=-1)
        onehot = topk_idx[:, :, None] == jnp.arange(NUM_EXPERTS)[None, None, :]
        w = jnp.sum(topk_probs[:, :, None] * onehot, axis=1)
        h = _gelu(jnp.einsum('td,edh->eth', xf, W1) + b1[:, None, :])
        y = jnp.einsum('eth,ehd->etd', h, W2) + b2[:, None, :]
        moe = jnp.einsum('te,etd->td', w, y)
        return (shared + moe).reshape(B, L, D)
    x = L0_attn_x
    x = x + 0.5 * _L0_ffn_ref(_layernorm(x, axis=-1), L0_ffn_rW, L0_ffn_rb, L0_ffn_W1, L0_ffn_b1, L0_ffn_W2, L0_ffn_b2, L0_ffn_sW1, L0_ffn_sb1, L0_ffn_sW2, L0_ffn_sb2)
    x = x + _L0_attn_ref(_layernorm(x, axis=-1), L0_attn_w_kv_down, L0_attn_w_kv_up, L0_attn_w_q, L0_attn_w_out)
    x = x + 0.5 * _L0_ffn_ref(_layernorm(x, axis=-1), L0_ffn_rW, L0_ffn_rb, L0_ffn_W1, L0_ffn_b1, L0_ffn_W2, L0_ffn_b2, L0_ffn_sW1, L0_ffn_sb1, L0_ffn_sW2, L0_ffn_sb2)
    return x

_drawn_inputs = setup_inputs


def setup_inputs(seed=0):
    import zlib

    import numpy as np

    out = dict(_drawn_inputs(seed))
    spreads = {'L0_ffn_rb': (0.0, 0.1),
     'L0_ffn_b1': (0.0, 0.465),
     'L0_ffn_b2': (0.0, 0.1),
     'L0_ffn_sb1': (0.0, 0.472),
     'L0_ffn_sb2': (0.0, 0.1)}
    factors = {'L0_attn_w_kv_down': 3.661,
     'L0_attn_w_kv_up': 3.688,
     'L0_attn_w_q': 8.0,
     'L0_attn_w_out': 3.715}
    for name, (base, spread) in spreads.items():
        noise = np.random.default_rng([zlib.crc32(name.encode()), seed]).standard_normal(out[name].shape)
        drawn = base * np.exp(spread * noise) if base else spread * noise
        out[name] = jnp.asarray(drawn.astype(out[name].dtype))
    for name, factor in factors.items():
        out[name] = (out[name] * factor).astype(out[name].dtype)
    return out
```

```python
from contextlib import ExitStack

import numpy as np

import concourse.bass as bass
from concourse import mybir

F32 = mybir.dt.float32
F32R = mybir.dt.float32r
BF16 = mybir.dt.bfloat16
ALU = mybir.AluOpType
ACT = mybir.ActivationFunctionType
AX = mybir.AxisListType

P = 128
BANK = 512
NEG = -1.0e30
BIG = 3.0e38
EPS = 1e-5

GQ = BANK // P


def head_steps(tiles):
    return [(g, j) for g in range(tiles // GQ) for j in range(GQ * g + GQ)]


def max_chunks(tiles):
    return [(i, c) for i in range(tiles) for c in range(i // GQ + 1)]


def macaron_kernel(nc, x, w_kv_down, w_kv_up, w_q, w_out, rW, rb, W1, b1, W2, b2, sW1, sb1, sW2, sb2, out):
    T, C = x.shape[1], x.shape[2]
    TILES = T // P
    GROUPS = T // BANK
    HD = w_q.shape[1]
    DH = 64
    PAIRS = HD // (2 * DH)
    E, _, HID = W1.shape
    S = sW1.shape[0]
    ALL = E + S
    HT = HID // P
    SCALE = float(DH) ** -0.5
    STEPS = head_steps(TILES)
    NS = len(STEPS)
    CHUNKS = max_chunks(TILES)
    NC = len(CHUNKS)
    MU = NC + 1
    assert C == P and TILES % GQ == 0 and NS % 4 == 0 and TILES * E == P
    UNIT_END = {STEPS.index((g, GQ * g + GQ - 1)): g for g in range(GROUPS)}

    CHUNK_FROM = {"A": 6, "B": 12}
    MAX_SLOT = {k: v + NC // 2 + 1 for k, v in CHUNK_FROM.items()}
    ROW_SLOT = {k: v + 1 for k, v in MAX_SLOT.items()}
    OUT_T = {13: 0, 15: 1, 27: 2}
    NORM_LAG = 2

    with ExitStack() as ctx:
        def sb(name, shape, dt=F32):
            return ctx.enter_context(nc.sbuf_tensor(name, shape, dt))

        def sem(name):
            return ctx.enter_context(nc.semaphore(name))

        bank = [ctx.enter_context(nc.psum_tensor(f"bank{i}", [P, BANK], F32)) for i in range(8)]

        resid = sb("resid", [P, TILES, P])
        xn = sb("xn", [P, TILES, P])
        latT = xn[:].rearrange("p a c -> p (a c)")
        xnT = sb("xnT", [P, T])
        xnT_hi = sb("xnT_hi", [P, T], F32R)
        xnT_lo = sb("xnT_lo", [P, T], F32R)
        qk_stage = sb("qk_stage", [P, 2, T])
        ypair = sb("ypair", [P, TILES, P])
        w1_hi = sb("w1_hi", [P, ALL, HID], F32R)
        w1_lo = sb("w1_lo", [P, ALL, HID], F32R)
        w2 = sb("w2", [P, ALL, HT, P])
        b1T = sb("b1T", [P, ALL, HT])
        b2_sb = sb("b2_sb", [E, P])
        sb2_all = sb("sb2_all", [P, S, P])
        rw_sb = sb("rw_sb", [P, E])
        rb_all = sb("rb_all", [P, E])
        hbuf = sb("hbuf", [P, 2 * HT, BANK])
        b1_rows = hbuf[0:ALL * HT, 2 * HT - 1, 0:P]
        stat = sb("stat", [P, 6, TILES])
        gate = sb("gate", [P, 8, TILES, E])
        rev = sb("rev", [P, E])
        wT = latT[0:E, :]
        minus_half = sb("minus_half", [P, TILES])
        ident = sb("ident", [P, P])
        ident_b = sb("ident_b", [P, P], BF16)
        mask_qk = sb("mask_qk", [P, P], BF16)
        mask_kq = sb("mask_kq", [P, P], BF16)
        wdown = sb("wdown", [P, P])
        wpair = sb("wpair", [P, 3, P])
        wo_pair = sb("wo_pair", [P, P])
        q_both = {"A": xnT_hi, "B": sb("q_both_B", [P, T], F32R)}
        q_hi_m = {h: sb(f"q_hi_m_{h}", [DH + 2, T], F32R) for h in "AB"}
        k_hi2 = {"A": xnT_lo, "B": sb("k_hi2_B", [P, T], F32R)}
        k_lo_1 = {h: sb(f"k_lo_1_{h}", [DH + 2, T], F32R) for h in "AB"}
        v_one = {h: sb(f"v_one_{h}", [P, TILES, DH + 1]) for h in "AB"}
        v_stage = hbuf[:, 5:7, :].rearrange("p a (b d) -> p (a b) d", d=DH)
        prob = hbuf[:, 0:4, :]
        yT = hbuf[:, 4, :]
        max_part = sb("max_part", [P, TILES, GROUPS])
        max_q = sb("max_q", [P, TILES])
        max_hi = sb("max_hi", [TILES, P], F32R)
        max_lo = sb("max_lo", [TILES, P], F32R)
        recip = sb("recip", [P, 2, GQ])
        HALF = {"A": (0, DH), "B": (DH, P)}
        OTHER = {"A": (DH, P), "B": (0, DH)}

        def w1_raw(e):
            if e < 2 * T // HID:
                return qk_stage[:].rearrange("p a t -> p (a t)")[:, e * HID:(e + 1) * HID]
            e -= 2 * T // HID
            return ypair[:].rearrange("p a t -> p (a t)")[:, e * HID:(e + 1) * HID]

        def max_bank(h, use):
            return bank[4 + ("AB".index(h) * MU + use) % 2]

        x_loaded, small_loaded, out_stored = sem("x_loaded"), sem("small_loaded"), sem("out_stored")
        w1_loaded = sem("w1_loaded")
        w2_loaded = sem("w2_loaded")
        pool_passed = sem("pool_passed")
        pool_step, consts_ready = sem("pool_step"), sem("consts_ready")
        dve_step = sem("dve_step")
        var_ready, rstd_ready, xn_ready = sem("var_ready"), sem("rstd_ready"), sem("xn_ready")
        xnT_mm, xnT_copied, xnT_split = sem("xnT_mm"), sem("xnT_copied"), sem("xnT_split")
        w1_hi_ready, w1_lo_ready = sem("w1_hi_ready"), sem("w1_lo_ready")
        gate_mm, gap_ready, gap_exp = sem("gate_mm"), sem("gap_ready"), sem("gap_exp")
        gate_ready, wT_mm, wT_copied, bias_mm = sem("gate_ready"), sem("wT_mm"), sem("wT_copied"), sem("bias_mm")
        b1_mm, b1T_ready = sem("b1_mm"), sem("b1T_ready")
        bias_read, rows_split, recip_done = (
            sem("bias_read"), sem("rows_split"), sem("recip_done"))
        h_mm, gelu_done, y_mm, y_added = sem("h_mm"), sem("gelu_done"), sem("y_mm"), sem("y_added")
        lat_mm, lat_copied = sem("lat_mm"), sem("lat_copied")
        wpair_loaded, wo_loaded = sem("wpair_loaded"), sem("wo_loaded")
        proj_mm, staged = sem("proj_mm"), sem("staged")
        hi_ready, v_ready, lo_ready, dup_loaded = sem("hi_ready"), sem("v_ready"), sem("lo_ready"), sem("dup_loaded")
        mx_mm, mx_read, max_ready = sem("mx_mm"), sem("mx_read"), sem("max_ready")
        rows_ready, rows_loaded = sem("rows_ready"), sem("rows_loaded")
        st_mm, exp_done, pv_mm, normed = sem("st_mm"), sem("exp_done"), sem("pv_mm"), sem("normed")
        yT_mm, yT_copied, op_mm, op_added = sem("yT_mm"), sem("yT_copied"), sem("op_mm"), sem("op_added")

        CR_GELU, CR_Y, CR_YA = HT, 2, 2
        CR_ST, CR_PV, CR_O, CR_MX, CR_OP = 2, 4, 2, 2, 1

        resid_flat = resid[:].rearrange("p a c -> p (a c)")
        x_tok = x.rearrange("o (a p) c -> p (o a) c", p=P)
        out_tok = out.rearrange("o (a p) c -> p (o a) c", p=P)
        block = ctx.enter_context(nc.Block())

        @block.sync
        def _(sp):
            sp.dma_start(resid[:], x_tok).then_inc(x_loaded, 16)
            sp.dma_start(rw_sb[:], rW).then_inc(small_loaded, 16)
            sp.dma_start(rb_all[:], rb.rearrange("(a e) -> a e", a=1).broadcast_to([P, E])).then_inc(small_loaded, 16)
            sp.dma_start(b1_rows[0:E * HT, :], b1.rearrange("e (h p) -> (e h) p", p=P)).then_inc(small_loaded, 16)
            sp.dma_start(b1_rows[E * HT:ALL * HT, :], sb1.rearrange("e (h p) -> (e h) p", p=P)).then_inc(small_loaded, 16)
            for e in range(ALL):
                src = W1[e] if e < E else sW1[e - E]
                sp.dma_start(w1_raw(e), src).then_inc(w1_loaded, 16)
            for s in range(S):
                sp.dma_start(sb2_all[:, s, :], sb2[s:s + 1, :].broadcast_to([P, P])).then_inc(small_loaded, 16)
            sp.dma_start(b2_sb[:], b2).then_inc(small_loaded, 16)
            sp.dma_start(wdown[:], w_kv_down).then_inc(small_loaded, 16)
            for e in range(ALL):
                src = W2[e] if e < E else sW2[e - E]
                sp.dma_start(w2[:, e, :, :], src.rearrange("(h p) d -> p h d", p=P)).then_inc(w2_loaded, 16)

            def load_wpair(pair):
                at = pair * P
                sp.dma_start(wpair[:, 0, :], w_q[:, bass.ds(at, P)]).then_inc(wpair_loaded, 16)
                sp.dma_start(wpair[:, 1, :], w_kv_up[:, bass.ds(at, P)]).then_inc(wpair_loaded, 16)
                sp.dma_start(wpair[:, 2, :], w_kv_up[:, bass.ds(at + HD, P)]).then_inc(wpair_loaded, 16)

            def duplicate(h, n):
                lo, hi = HALF[h]
                o_lo, o_hi = OTHER[h]
                sp.wait_ge(hi_ready, 2 * n + 1)
                sp.dma_start(k_hi2[h][o_lo:o_hi, :].bitcast(F32), k_hi2[h][lo:hi, :].bitcast(F32)).then_inc(dup_loaded, 16)
                sp.wait_ge(hi_ready, 2 * n + 2)
                sp.dma_start(q_hi_m[h][0:DH, :].bitcast(F32), q_both[h][lo:hi, :].bitcast(F32)).then_inc(dup_loaded, 16)

            def max_rows(h, n):
                sp.wait_ge(rows_ready, n + 1)
                sp.dma_start(q_hi_m[h][DH:DH + 1, :].bitcast(F32), max_hi[:].bitcast(F32)).then_inc(rows_loaded, 16)
                sp.dma_start(q_hi_m[h][DH + 1:DH + 2, :].bitcast(F32), max_lo[:].bitcast(F32)).then_inc(rows_loaded, 16)

            load_wpair(0)
            duplicate("A", 0)
            max_rows("A", 0)

            def pair_body(p, last=False):
                sp.wait_ge(op_added, GROUPS * p + CR_OP)
                sp.dma_start(wo_pair[:], w_out[bass.ds(p * P, P), :]).then_inc(wo_loaded, 16)
                if not last:
                    sp.wait_ge(proj_mm, 12 * p + 12)
                    load_wpair(p + 1)
                duplicate("B", 2 * p + 1)
                max_rows("B", 2 * p + 1)
                if not last:
                    duplicate("A", 2 * p + 2)
                    max_rows("A", 2 * p + 2)

            with sp.Fori(0, PAIRS - 1) as p:
                pair_body(p)
            pair_body(PAIRS - 1, last=True)

            sp.wait_ge(y_added, CR_YA + 2 * GROUPS * ALL)
            sp.dma_start(out_tok, resid[:]).then_inc(out_stored, 16)
            sp.wait_ge(out_stored, 16)

        @block.gpsimd
        def _(pool):
            pool.memset(ident[:], 0.0).then_inc(pool_step, 1)
            pool.memset(mask_qk[:], 0.0).then_inc(pool_step, 1)
            pool.memset(mask_kq[:], 0.0).then_inc(pool_step, 1)
            pool.memset(minus_half[:], -0.5).then_inc(pool_step, 1)
            pool.wait_ge(pool_step, 4)
            pool.affine_select(out=ident[:], in_=ident[:], compare_op=ALU.not_equal, fill=1.0, base=0,
                               pattern=[[-1, P]], channel_multiplier=1).then_inc(pool_step, 1)
            pool.affine_select(out=mask_qk[:], in_=mask_qk[:], compare_op=ALU.is_ge, fill=NEG, base=0,
                               pattern=[[-1, P]], channel_multiplier=1).then_inc(pool_step, 1)
            pool.affine_select(out=mask_kq[:], in_=mask_kq[:], compare_op=ALU.is_ge, fill=NEG, base=0,
                               pattern=[[1, P]], channel_multiplier=-1).then_inc(pool_step, 1)
            pool.wait_ge(pool_step, 7)
            for h in "AB":
                pool.memset(k_lo_1[h][DH:DH + 2, :].bitcast(F32), -1.0).then_inc(pool_step, 1)
                pool.wait_ge(pool_step, 8 + 2 * "AB".index(h))
                pool.memset(v_one[h][:, :, DH:DH + 1], 1.0).then_inc(pool_step, 1)
                pool.wait_ge(pool_step, 9 + 2 * "AB".index(h))
            for e in range(E):
                pool.memset(rev[:, e:e + 1], float(E - e)).then_inc(pool_step, 1)
            pool.wait_ge(pool_step, 11 + E)
            pool.tensor_copy(ident_b[:], ident[:]).then_inc(consts_ready, 1)

            def rstd(norm):
                pool.wait_ge(var_ready, norm + 1)
                pool.tensor_tensor(stat[:, 4, :], stat[:, 3, :], minus_half[:], ALU.pow).then_inc(rstd_ready, 1)

            def split_hi(h, n, pair):
                lo, hi = HALF[h]
                pool.wait_ge(staged, 12 * pair + 8)
                pool.sem_inc(pool_passed, 1)
                pool.tensor_copy(k_hi2[h][lo:hi, :], qk_stage[lo:hi, 1, :]).then_inc(hi_ready, 1)
                pool.wait_ge(hi_ready, 2 * n + 1)
                pool.sem_inc(pool_passed, 1)
                pool.tensor_copy(q_both[h][lo:hi, :], qk_stage[lo:hi, 0, :]).then_inc(hi_ready, 1)
                pool.wait_ge(hi_ready, 2 * n + 2)
                pool.sem_inc(pool_passed, 1)

            rstd(0)
            rstd(1)
            split_hi("A", 0, 0)

            def pair_body(p, last=False):
                pool.wait_ge(st_mm, 2 * NS * p + 1)
                split_hi("B", 2 * p + 1, p)
                pool.wait_ge(pv_mm, 2 * NS * p + CR_PV)
                pool.wait_ge(staged, 12 * p + 12)
                pool.sem_inc(pool_passed, 1)
                pool.tensor_copy(v_one["B"][:, :, 0:DH], v_stage[:]).then_inc(v_ready, 1)
                pool.wait_ge(v_ready, p + 1)
                pool.sem_inc(pool_passed, 1)
                if not last:
                    pool.wait_ge(st_mm, 2 * NS * p + NS)
                    split_hi("A", 2 * p + 2, p + 1)

            with pool.Fori(0, PAIRS - 1) as p:
                pair_body(p)
            pair_body(PAIRS - 1, last=True)
            rstd(2)

        @block.scalar
        def _(act):
            act.sem_inc(gelu_done, CR_GELU)
            act.sem_inc(exp_done, CR_ST)

            def copy_xnT(norm):
                for g in range(GROUPS):
                    act.wait_ge(xnT_mm, GROUPS * norm + g + 1)
                    act.activation(xnT[:, g * BANK:(g + 1) * BANK], bank[g][:], ACT.Copy).then_inc(xnT_copied, 1)

            def ffn(f):
                copy_xnT(2 * f)
                if f == 0:
                    for e in range(ALL):
                        act.wait_ge(w1_loaded, 16 * ALL)
                        act.activation(w1_hi[:, e, :], w1_raw(e), ACT.Copy).then_inc(w1_hi_ready, 1)
                act.wait_ge(gap_ready, f + 1)
                act.activation(gate[:, 7, :, 0], stat[:, 0, :], ACT.Exp).then_inc(gap_exp, 1)
                for g in range(GROUPS):
                    act.wait_ge(wT_mm, GROUPS * f + g + 1)
                    act.activation(wT[:, g * BANK:(g + 1) * BANK], bank[g][0:E, :], ACT.Copy).then_inc(wT_copied, 1)
                act.wait_ge(b1T_ready, 1)
                with act.Fori(0, GROUPS) as g:
                    for e in range(ALL):
                        y_at = (f * GROUPS + g) * ALL + e
                        act.wait_ge(y_mm, y_at - 2 + 1 + CR_Y)
                        for ht in range(HT):
                            act.wait_ge(h_mm, y_at * HT + ht + 1)
                            act.activation(hbuf[:, e % 2 * HT + ht, :], bank[ht][:], ACT.Gelu,
                                           bias=b1T[:, e, ht:ht + 1]).then_inc(gelu_done, 1)

            ffn(0)

            copy_xnT(1)
            for g in range(GROUPS):
                act.wait_ge(lat_mm, g + 1)
                act.activation(latT[:, g * BANK:(g + 1) * BANK], bank[4 + g][:], ACT.Copy).then_inc(lat_copied, 1)

            def stage(pair, k):
                act.wait_ge(proj_mm, 12 * pair + k + 1)
                src = bank[6 + k % 2]
                if k < 8:
                    act.activation(qk_stage[:, k // 4, k % 4 * BANK:(k % 4 + 1) * BANK], src[:], ACT.Copy)\
                       .then_inc(staged, 1)
                else:
                    tiles = slice(GQ * (k - 8), GQ * (k - 8) + GQ)
                    v = src[:].rearrange("p (a d) -> p a d", a=GQ)
                    act.activation(v_one["A"][:, tiles, 0:DH], v[:, :, 0:DH], ACT.Copy)
                    act.activation(v_stage[:, tiles, :], v[:, :, DH:P], ACT.Copy).then_inc(staged, 1)

            for k in range(12):
                stage(0, k)

            def copy_yT(p, g):
                act.wait_ge(yT_mm, GROUPS * p + g + 1)
                act.activation(yT, bank[6][:], ACT.Copy).then_inc(yT_copied, 1)

            def pair_body(p, last=False):
                for n in range(2 * NS):
                    s = n % NS
                    g, j = STEPS[s]
                    at = max(GQ * g, j)
                    width = (GQ * g + GQ - at) * P
                    act.wait_ge(st_mm, 2 * NS * p + n + 1)
                    act.wait_ge(pv_mm, 2 * NS * p + n + 1)
                    act.activation(prob[:, n % 4, 0:width], bank[n % 2][:, 0:width], ACT.Exp, scale=SCALE)\
                       .then_inc(exp_done, 1)
                    if n >= NS:
                        if s < 12 and not last:
                            if s == 0:
                                act.wait_ge(hi_ready, 4 * p + 4)
                                act.wait_ge(lo_ready, 4 * p + 4)
                            if s == 8:
                                act.wait_ge(v_ready, p + 1)
                            stage(p + 1, s)
                        if s in OUT_T:
                            copy_yT(p, OUT_T[s])
                copy_yT(p, GROUPS - 1)

            with act.Fori(0, PAIRS - 1) as p:
                pair_body(p)
            pair_body(PAIRS - 1, last=True)
            ffn(1)

        @block.vector
        def _(dve):
            step = [0]

            def link(ins):
                step[0] += 1
                ins.then_inc(dve_step, 1)
                dve.wait_ge(dve_step, step[0])

            def over_channels(ap):
                return ap.rearrange("p (a o) -> p a o", o=1).broadcast_to([P, TILES, P])

            def over_experts(ap):
                return ap.rearrange("p (a o) -> p a o", o=1).broadcast_to([P, TILES, E])

            def norm(n):
                link(dve.reduce_sum(stat[:, 1, :], resid[:], axis=AX.X))
                link(dve.tensor_scalar(stat[:, 2, :], stat[:, 1, :], 1.0 / C, None, ALU.mult))
                link(dve.tensor_tensor(xn[:], resid[:], over_channels(stat[:, 2, :]), ALU.subtract))
                square = xnT[:].rearrange("p (a c) -> p a c", c=P)
                link(dve.tensor_tensor(square, xn[:], xn[:], ALU.mult))
                link(dve.reduce_sum(stat[:, 1, :], square, axis=AX.X))
                dve.tensor_scalar(stat[:, 3, :], stat[:, 1, :], 1.0 / C, EPS, ALU.mult, ALU.add).then_inc(var_ready, 1)
                dve.wait_ge(rstd_ready, n + 1)
                dve.tensor_tensor(xn[:], xn[:], over_channels(stat[:, 4, :]), ALU.mult).then_inc(xn_ready, 1)

            def split_xnT(n):
                dve.wait_ge(xnT_copied, GROUPS * (n + 1))
                link(dve.tensor_copy(xnT_hi[:], xnT[:]))
                dve.tensor_tensor(xnT_lo[:], xnT[:], xnT_hi[:].bitcast(F32), ALU.subtract).then_inc(xnT_split, 1)

            def ffn(f):
                norm(2 * f)
                split_xnT(2 * f)
                if f == 0:
                    for e in range(ALL):
                        dve.wait_ge(w1_hi_ready, e + 1)
                        dve.tensor_tensor(w1_lo[:, e, :], w1_raw(e), w1_hi[:, e, :].bitcast(F32), ALU.subtract)\
                           .then_inc(w1_lo_ready, 1)
                G, EQ, KEY, OH1, G2, OH2, W, TMP = range(8)
                dve.wait_ge(gate_mm, f + 1)
                gates = bank[4][:, 0:TILES * E].rearrange("p (a e) -> p a e", e=E)
                rb_b = rb_all[:].rearrange("p (o e) -> p o e", o=1).broadcast_to([P, TILES, E])
                rev_b = rev[:].rearrange("p (o e) -> p o e", o=1).broadcast_to([P, TILES, E])
                link(dve.tensor_tensor(gate[:, G], gates, rb_b, ALU.add))
                for src, best, onehot in ((G, 1, OH1), (G2, 2, OH2)):
                    if src == G2:
                        link(dve.scalar_tensor_tensor(out=gate[:, G2], in0=gate[:, OH1], scalar=-BIG,
                                                      in1=gate[:, G], op0=ALU.mult, op1=ALU.add))
                    link(dve.reduce_max(stat[:, best, :], gate[:, src], axis=AX.X))
                    link(dve.tensor_tensor(gate[:, EQ], gate[:, src], over_experts(stat[:, best, :]), ALU.is_equal))
                    link(dve.tensor_tensor(gate[:, KEY], gate[:, EQ], rev_b, ALU.mult))
                    link(dve.reduce_max(stat[:, 5, :], gate[:, KEY], axis=AX.X))
                    link(dve.tensor_tensor(gate[:, onehot], gate[:, KEY], over_experts(stat[:, 5, :]), ALU.is_equal))
                dve.tensor_tensor(stat[:, 0, :], stat[:, 2, :], stat[:, 1, :], ALU.subtract).then_inc(gap_ready, 1)
                dve.wait_ge(gap_exp, f + 1)
                ex = gate[:, TMP, :, 0]
                link(dve.tensor_scalar(stat[:, 3, :], ex, 1.0, None, ALU.add))
                link(dve.reciprocal(stat[:, 5, :], stat[:, 3, :]))
                link(dve.tensor_scalar(stat[:, 1, :], stat[:, 5, :], 0.5, None, ALU.mult))
                link(dve.tensor_tensor(stat[:, 2, :], ex, stat[:, 1, :], ALU.mult))
                link(dve.tensor_tensor(gate[:, EQ], gate[:, OH1], over_experts(stat[:, 1, :]), ALU.mult))
                link(dve.tensor_tensor(gate[:, KEY], gate[:, OH2], over_experts(stat[:, 2, :]), ALU.mult))
                dve.tensor_tensor(gate[:, W], gate[:, EQ], gate[:, KEY], ALU.add).then_inc(gate_ready, 1)
                if f == 0:
                    dve.wait_ge(b1_mm, 1)
                    dve.tensor_copy(b1T[:].rearrange("p e h -> p (e h)"), bank[5][:, 0:ALL * HT]).then_inc(b1T_ready, 1)
                    dve.wait_ge(small_loaded, 16 * (6 + S))
                    link(dve.tensor_tensor(sb2_all[:, 0, :], sb2_all[:, 0, :], sb2_all[:, 1, :], ALU.add))
                shared = sb2_all[:, 0:1, :].broadcast_to([P, TILES, P])
                link(dve.scalar_tensor_tensor(out=resid[:], in0=shared, scalar=0.5 / S, in1=resid[:],
                                              op0=ALU.mult, op1=ALU.add))
                for g in range(GROUPS):
                    dve.wait_ge(bias_mm, GROUPS * f + g + 1)
                    part = resid_flat[:, g * BANK:(g + 1) * BANK]
                    dve.tensor_tensor(part, bank[6 + g % 2][:], part, ALU.add).then_inc(bias_read, 1)
                dve.wait_ge(bias_read, GROUPS * (f + 1))
                dve.wait_ge(gate_ready, f + 1)
                with dve.Fori(0, GROUPS) as g:
                    for e in range(ALL):
                        y_at = (f * GROUPS + g) * ALL + e
                        dve.wait_ge(y_mm, y_at + 1 + CR_Y)
                        dve.wait_ge(y_added, y_at + CR_YA)
                        for t in range(GQ):
                            part = resid[:, bass.ds(g * GQ + t, 1), :].rearrange("p o c -> p (o c)")
                            weight = 0.5 / S if e >= E else \
                                gate[:, W, bass.ds(g * GQ + t, 1), e:e + 1].rearrange("p o e -> p (o e)")
                            ins = dve.scalar_tensor_tensor(
                                out=part, in0=bank[6 + e % 2][:, t * P:(t + 1) * P], scalar=weight, in1=part,
                                op0=ALU.mult, op1=ALU.add)
                        ins.then_inc(y_added, 1)
                dve.wait_ge(y_added, (f + 1) * GROUPS * ALL + CR_YA)

            dve.sem_inc(y_added, CR_YA)
            dve.sem_inc(normed, CR_O)
            dve.sem_inc(mx_read, CR_MX)
            dve.sem_inc(op_added, CR_OP)
            dve.wait_ge(x_loaded, 16)
            dve.wait_ge(consts_ready, 1)
            ffn(0)
            norm(1)
            link(dve.memset(max_part[:], -BIG))

            def split_lo(h, n):
                lo, hi = HALF[h]
                o_lo, o_hi = OTHER[h]
                dve.wait_ge(hi_ready, 2 * n + 1)
                dve.tensor_tensor(k_lo_1[h][0:DH, :], qk_stage[lo:hi, 1, :], k_hi2[h][lo:hi, :].bitcast(F32),
                                  ALU.subtract).then_inc(lo_ready, 1)
                dve.wait_ge(hi_ready, 2 * n + 2)
                dve.tensor_tensor(q_both[h][o_lo:o_hi, :], qk_stage[lo:hi, 0, :], q_both[h][lo:hi, :].bitcast(F32),
                                  ALU.subtract).then_inc(lo_ready, 1)

            def reduce_chunk(h, n, c):
                i, part = CHUNKS[c]
                width = min(BANK, (i + 1) * P - part * BANK)
                dve.wait_ge(mx_mm, MU * n + c + 1)
                dve.reduce_max(max_part[:, i, part:part + 1], max_bank(h, c)[:, 0:width], axis=AX.X)\
                   .then_inc(mx_read, 1)

            def reduce_last(n):
                dve.wait_ge(mx_read, MU * n + NC + CR_MX)
                dve.reduce_max(max_q[:], max_part[:], axis=AX.X).then_inc(max_ready, 1)

            def split_rows(h, n, first=False):
                src = max_bank(h, NC)[0:TILES, 0:P]
                dve.wait_ge(mx_mm, MU * n + NC + 1)
                if not first:
                    dve.wait_ge(rows_loaded, 32 * n)
                dve.tensor_copy(max_hi[:], src).then_inc(rows_split, 1)
                dve.wait_ge(rows_split, n + 1)
                dve.tensor_tensor(max_lo[:], src, max_hi[:].bitcast(F32), ALU.subtract).then_inc(mx_read, 1)
                dve.wait_ge(mx_read, MU * n + MU + CR_MX)
                dve.sem_inc(rows_ready, 1)

            def normalise(p, head, g):
                u = GROUPS * head + g
                last_step = NS * head + STEPS.index((g, GQ * g + GQ - 1))
                o = bank[2 + u % 2][:, 0:GQ * (DH + 1)].rearrange("p (a d) -> p a d", d=DH + 1)
                dve.wait_ge(pv_mm, 2 * NS * p + last_step + 1 + CR_PV)
                dve.reciprocal(recip[:, u % 2, :], o[:, :, DH]).then_inc(recip_done, 1)
                dve.wait_ge(recip_done, 2 * GROUPS * p + u + 1)
                r = recip[:, u % 2, :].rearrange("p (a o) -> p a o", o=1).broadcast_to([P, GQ, DH])
                dve.tensor_tensor(ypair[:, GQ * g:GQ * g + GQ, DH * head:DH * head + DH], o[:, :, 0:DH], r, ALU.mult)\
                   .then_inc(normed, 1)

            def add_out(p, g):
                dve.wait_ge(op_mm, GROUPS * p + g + 1)
                part = resid_flat[:, g * BANK:(g + 1) * BANK]
                dve.tensor_tensor(part, bank[7][:], part, ALU.add).then_inc(op_added, 1)

            split_lo("A", 0)
            for c in range(NC):
                reduce_chunk("A", 0, c)
            reduce_last(0)
            split_rows("A", 0, first=True)

            def pair_body(p, last=False):
                for n in range(2 * NS):
                    s, head = n % NS, n // NS
                    here, nxt = "AB"[head], "BA"[head]
                    number = 2 * p + 1 + head
                    if not (last and head == 1):
                        if s == (0, 8)[head]:
                            split_lo(nxt, number)
                        for c in range(2 * (s - CHUNK_FROM[here]), 2 * (s - CHUNK_FROM[here]) + 2):
                            if 0 <= c < NC:
                                reduce_chunk(nxt, number, c)
                        if s == MAX_SLOT[here]:
                            reduce_last(number)
                        if s == ROW_SLOT[here]:
                            split_rows(nxt, number)
                    ended = n - NORM_LAG
                    if ended >= 0 and ended % NS in UNIT_END:
                        normalise(p, ended // NS, UNIT_END[ended % NS])
                    if head == 1 and s - 1 in OUT_T:
                        add_out(p, OUT_T[s - 1])
                normalise(p, 1, GROUPS - 1)
                add_out(p, GROUPS - 1)

            with dve.Fori(0, PAIRS - 1) as p:
                pair_body(p)
            pair_body(PAIRS - 1, last=True)
            dve.wait_ge(op_added, GROUPS * PAIRS + CR_OP)
            ffn(1)

        @block.tensor
        def _(pe):
            pe.sem_inc(y_mm, CR_Y)
            pe.sem_inc(pv_mm, CR_PV)

            def three_pass(dst, l_hi, l_lo, r_hi, r_lo):
                pe.matmul(dst, l_hi, r_hi, start=True, stop=False)
                pe.matmul(dst, l_hi, r_lo, start=False, stop=False)
                return pe.matmul(dst, l_lo, r_hi, start=False, stop=True)

            def transpose_xn(n):
                pe.wait_ge(xn_ready, n + 1)
                for g in range(GROUPS):
                    for t in range(GQ):
                        ins = pe.transpose(bank[g][:, t * P:(t + 1) * P], xn[:, g * GQ + t, :], ident[:])
                    ins.then_inc(xnT_mm, 1)

            def ffn(f):
                transpose_xn(2 * f)
                pe.wait_ge(xnT_copied, GROUPS * (2 * f + 1))
                if f == 0:
                    pe.wait_ge(small_loaded, 16 * (6 + S))
                    pe.transpose(bank[5][:, 0:ALL * HT], b1_rows, ident[0:ALL * HT, 0:ALL * HT]).then_inc(b1_mm, 1)
                for t in range(TILES):
                    ins = pe.matmul(bank[4][:, t * E:(t + 1) * E], xnT[:, t * P:(t + 1) * P], rw_sb[:],
                                    start=True, stop=True)
                ins.then_inc(gate_mm, 1)
                pe.wait_ge(gate_ready, f + 1)
                for g in range(GROUPS):
                    for t in range(GQ):
                        ins = pe.transpose(bank[g][0:E, t * P:(t + 1) * P], gate[:, 6, g * GQ + t, :], ident[:])
                    ins.then_inc(wT_mm, 1)
                pe.wait_ge(wT_copied, GROUPS * (f + 1))
                for g in range(GROUPS):
                    if g >= 2:
                        pe.wait_ge(bias_read, GROUPS * f + g - 1)
                    for t in range(GQ):
                        tile = g * GQ + t
                        ins = pe.matmul(bank[6 + g % 2][:, t * P:(t + 1) * P], wT[:, tile * P:(tile + 1) * P],
                                        b2_sb[:], start=True, stop=True)
                    ins.then_inc(bias_mm, 1)
                pe.wait_ge(bias_read, GROUPS * (f + 1))
                pe.wait_ge(xnT_split, f + 1)
                if f == 0:
                    pe.wait_ge(w1_lo_ready, ALL)
                    pe.wait_ge(w2_loaded, 16 * ALL)

                def second_layer(g, e):
                    y_at = (f * GROUPS + g) * ALL + e
                    pe.wait_ge(gelu_done, y_at * HT + HT + CR_GELU)
                    pe.wait_ge(y_added, y_at - 2 + 1 + CR_YA)
                    for t in range(GQ):
                        for ht in range(HT):
                            ins = pe.matmul(bank[6 + e % 2][:, t * P:(t + 1) * P],
                                            hbuf[:, e % 2 * HT + ht, t * P:(t + 1) * P], w2[:, e, ht, :],
                                            start=ht == 0, stop=ht == HT - 1)
                    ins.then_inc(y_mm, 1)

                with pe.Fori(0, GROUPS) as g:
                    x_hi = xnT_hi[:, bass.ds(g * BANK, BANK)]
                    x_lo = xnT_lo[:, bass.ds(g * BANK, BANK)]
                    for e in range(ALL):
                        for ht in range(HT):
                            at = ((f * GROUPS + g) * ALL + e) * HT + ht
                            pe.wait_ge(gelu_done, at - HT + 1 + CR_GELU)
                            cols = slice(ht * P, (ht + 1) * P)
                            three_pass(bank[ht][:], w1_hi[:, e, cols], w1_lo[:, e, cols], x_hi, x_lo)\
                                .then_inc(h_mm, 1)
                        if e >= 1:
                            second_layer(g, e - 1)
                    second_layer(g, ALL - 1)

            pe.wait_ge(consts_ready, 1)
            ffn(0)

            transpose_xn(1)
            pe.wait_ge(xnT_copied, 2 * GROUPS)
            pe.wait_ge(y_added, GROUPS * ALL + CR_YA)
            for g in range(GROUPS):
                pe.matmul(bank[4 + g][:], wdown[:], xnT[:, g * BANK:(g + 1) * BANK], start=True, stop=True)\
                  .then_inc(lat_mm, 1)
            pe.wait_ge(lat_copied, GROUPS)

            def project(pair, k):
                dst = bank[6 + k % 2]
                if k == 0:
                    pe.wait_ge(wpair_loaded, 48 * pair + 48)
                if k < 8:
                    src = xnT if k < 4 else latT
                    pe.matmul(dst[:], wpair[:, k // 4, :], src[:, k % 4 * BANK:(k % 4 + 1) * BANK],
                              start=True, stop=True).then_inc(proj_mm, 1)
                else:
                    for t in range(GQ):
                        tile = GQ * (k - 8) + t
                        ins = pe.matmul(dst[:, t * P:(t + 1) * P], latT[:, tile * P:(tile + 1) * P], wpair[:, 2, :],
                                        start=True, stop=True)
                    ins.then_inc(proj_mm, 1)

            def max_chunk(h, n, c):
                i, part = CHUNKS[c]
                lo, hi = HALF[h]
                width = min(BANK, (i + 1) * P - part * BANK)
                diagonal = part == i // GQ
                dst = max_bank(h, c)
                pe.wait_ge(mx_read, MU * n + c - 2 + 1 + CR_MX)
                ins = pe.matmul(dst[:, 0:width], q_both[h][lo:hi, i * P:(i + 1) * P],
                                k_hi2[h][lo:hi, part * BANK:part * BANK + width], start=True, stop=not diagonal)
                if diagonal:
                    ins = pe.matmul(dst[:, width - P:width], ident_b[:], mask_qk[:], start=False, stop=True)
                ins.then_inc(mx_mm, 1)

            def max_transpose(h, n):
                pe.wait_ge(max_ready, n + 1)
                pe.wait_ge(mx_read, MU * n + NC - 2 + 1 + CR_MX)
                pe.transpose(max_bank(h, NC)[0:TILES, 0:P], max_q[:], ident[:]).then_inc(mx_mm, 1)

            for k in range(12):
                if k >= 2:
                    pe.wait_ge(staged, k - 1)
                project(0, k)
            pe.wait_ge(hi_ready, 2)
            for c in range(NC):
                max_chunk("A", 0, c)
            max_transpose("A", 0)

            def scores(p, n):
                head, s = n // NS, n % NS
                h = "AB"[head]
                g, j = STEPS[s]
                at = max(GQ * g, j)
                width = (GQ * g + GQ - at) * P
                keys, queries = slice(j * P, (j + 1) * P), slice(at * P, at * P + width)
                diagonal = j >= GQ * g
                dst = bank[n % 2]
                if s == 0:
                    number = 2 * p + head
                    pe.wait_ge(lo_ready, 2 * number + 2)
                    pe.wait_ge(dup_loaded, 32 * number + 32)
                    pe.wait_ge(rows_loaded, 32 * number + 32)
                pe.wait_ge(exp_done, 2 * NS * p + n - 2 + 1 + CR_ST)
                pe.matmul(dst[:, 0:width], k_hi2[h][:, keys], q_both[h][:, queries], start=True, stop=False)
                ins = pe.matmul(dst[:, 0:width], k_lo_1[h][:, keys], q_hi_m[h][:, queries],
                                start=False, stop=not diagonal)
                if diagonal:
                    ins = pe.matmul(dst[:, 0:P], ident_b[:], mask_kq[:], start=False, stop=True)
                ins.then_inc(st_mm, 1)

            def weigh(p, n):
                head, s = n // NS, n % NS
                g, j = STEPS[s]
                at = max(GQ * g, j)
                u = GROUPS * head + g
                if j == 0:
                    pe.wait_ge(normed, 2 * GROUPS * p + u - 2 + 1 + CR_O)
                if s == 0 and head == 1:
                    pe.wait_ge(v_ready, p + 1)
                if s == 0 and head == 0:
                    pe.wait_ge(staged, 12 * p + 12)
                pe.wait_ge(exp_done, 2 * NS * p + n + 1 + CR_ST)
                for i in range(at, GQ * g + GQ):
                    t = i - GQ * g
                    ins = pe.matmul(bank[2 + u % 2][:, t * (DH + 1):(t + 1) * (DH + 1)],
                                    prob[:, n % 4, (i - at) * P:(i - at + 1) * P], v_one["AB"[head]][:, j, :],
                                    start=j == 0 and t == 0, stop=j == i, skip_group_check=True)
                ins.then_inc(pv_mm, 1)

            def out_transpose(p, g):
                pe.wait_ge(normed, 2 * GROUPS * p + GROUPS + g + 1 + CR_O)
                for t in range(GQ):
                    ins = pe.transpose(bank[6][:, t * P:(t + 1) * P], ypair[:, g * GQ + t, :], ident[:])
                ins.then_inc(yT_mm, 1)

            def out_project(p, g):
                pe.wait_ge(yT_copied, GROUPS * p + g + 1)
                pe.wait_ge(op_added, GROUPS * p + g + CR_OP)
                for t in range(GQ):
                    ins = pe.matmul(bank[7][:, t * P:(t + 1) * P], yT[:, t * P:(t + 1) * P], wo_pair[:],
                                    start=True, stop=True)
                ins.then_inc(op_mm, 1)

            def pair_body(p, last=False):
                for n in range(2 * NS):
                    s, head = n % NS, n // NS
                    here, nxt = "AB"[head], "BA"[head]
                    number = 2 * p + 1 + head
                    scores(p, n)
                    if not (last and head == 1):
                        if head == 1 and s < 12:
                            if s == 1:
                                pe.wait_ge(op_added, GROUPS * p + CR_OP)
                            if s >= 2:
                                pe.wait_ge(staged, 12 * p + 12 + s - 1)
                            project(p + 1, s)
                        if s == CHUNK_FROM[here]:
                            pe.wait_ge(hi_ready, 2 * number + 2)
                        for c in range(2 * (s - CHUNK_FROM[here]), 2 * (s - CHUNK_FROM[here]) + 2):
                            if 0 <= c < NC:
                                max_chunk(nxt, number, c)
                        if s == ROW_SLOT[here]:
                            max_transpose(nxt, number)
                    if n >= 1:
                        weigh(p, n - 1)
                    if head == 1:
                        if s == 13:
                            if not last:
                                pe.wait_ge(staged, 12 * p + 24)
                            pe.wait_ge(wo_loaded, 16 * p + 16)
                        if s in OUT_T:
                            out_transpose(p, OUT_T[s])
                        if s - 1 in OUT_T:
                            out_project(p, OUT_T[s - 1])
                weigh(p, 2 * NS - 1)
                out_transpose(p, GROUPS - 1)
                out_project(p, GROUPS - 1)

            with pe.Fori(0, PAIRS - 1) as p:
                pair_body(p)
            pair_body(PAIRS - 1, last=True)
            ffn(1)


_INS = ["L0_attn_x", "L0_attn_w_kv_down", "L0_attn_w_kv_up", "L0_attn_w_q", "L0_attn_w_out", "L0_ffn_rW",
        "L0_ffn_rb", "L0_ffn_W1", "L0_ffn_b1", "L0_ffn_W2", "L0_ffn_b2", "L0_ffn_sW1", "L0_ffn_sb1",
        "L0_ffn_sW2", "L0_ffn_sb2"]


def kernel(**inputs):
    import concourse.bacc as _bacc
    from concourse.bass_utils import run_bass_kernel_spmd as _run

    nc = _bacc.Bacc("TRN2", target_bir_lowering=False, num_devices=1)
    arrays, args = {}, []
    for name in _INS:
        a = np.ascontiguousarray(inputs[name])
        arrays[f"in_{name}"] = a
        args.append(nc.dram_tensor(f"in_{name}", a.shape, mybir.dt.from_np(a.dtype), kind="ExternalInput").ap())
    shape = inputs["L0_attn_x"].shape
    args.append(nc.dram_tensor("out_x", shape, F32, kind="ExternalOutput").ap())
    macaron_kernel(nc, *args)
    r = _run(nc, [arrays], core_ids=[0])
    return r.results[0]["out_x"]
```

```python
from contextlib import ExitStack

import numpy as np

import concourse.bass as bass
from concourse import mybir

F32 = mybir.dt.float32
F32R = mybir.dt.float32r
BF16 = mybir.dt.bfloat16
ALU = mybir.AluOpType
ACT = mybir.ActivationFunctionType
AX = mybir.AxisListType

P = 128
BANK = 512
NEG = -1.0e30
BIG = 3.0e38
EPS = 1e-5

GQ = BANK // P


def head_steps(tiles):
    return [(g, j) for g in range(tiles // GQ) for j in range(GQ * g + GQ)]


def max_chunks(tiles):
    return [(i, c) for i in range(tiles) for c in range(i // GQ + 1)]


def macaron_kernel(nc, x, w_kv_down, w_kv_up, w_q, w_out, rW, rb, W1, b1, W2, b2, sW1, sb1, sW2, sb2, out):
    T, C = x.shape[1], x.shape[2]
    TILES = T // P
    GROUPS = T // BANK
    HD = w_q.shape[1]
    DH = 64
    PAIRS = HD // (2 * DH)
    E, _, HID = W1.shape
    S = sW1.shape[0]
    ALL = E + S
    HT = HID // P
    SCALE = float(DH) ** -0.5
    STEPS = head_steps(TILES)
    NS = len(STEPS)
    CHUNKS = max_chunks(TILES)
    NC = len(CHUNKS)
    MU = NC + 1
    assert C == P and TILES % GQ == 0 and NS % 4 == 0 and TILES * E == P
    UNIT_LAST = [STEPS.index((g, GQ * g + GQ - 1)) for g in range(GROUPS)]

    def unit_ended(n):
        head, s = n // NS, n % NS
        return GROUPS * head + UNIT_LAST.index(s) if s in UNIT_LAST else None


    PIECES = 2 * (T // BANK)
    PIECE_SLOTS = {"A": [[2 * i, 2 * i + 1] for i in range(PIECES // 2)], "B": [[i] for i in range(PIECES)]}
    PROJ = PIECES + T // BANK
    CHUNK_FROM = {"A": 5, "B": 9}
    MAX_SLOT = {k: v + NC // 2 for k, v in CHUNK_FROM.items()}
    ROW_SLOT = {k: v + 1 for k, v in MAX_SLOT.items()}
    COPY_LAG = 2
    ROUNDS = 2
    RT = GQ // ROUNDS

    with ExitStack() as ctx:
        def sb(name, shape, dt=F32):
            return ctx.enter_context(nc.sbuf_tensor(name, shape, dt))

        def sem(name):
            return ctx.enter_context(nc.semaphore(name))

        bank = [ctx.enter_context(nc.psum_tensor(f"bank{i}", [P, BANK], F32)) for i in range(8)]

        resid = sb("resid", [P, TILES, P])
        xn = sb("xn", [P, TILES, P])
        latT = xn[:].rearrange("p a c -> p (a c)")
        xnT = sb("xnT", [P, T])
        xnT_hi = sb("xnT_hi", [P, T], F32R)
        xnT_lo = sb("xnT_lo", [P, T], F32R)
        qk_stage = sb("qk_stage", [P, 2, T])
        w1_rest = sb("w1_rest", [P, TILES, P])
        w1_hi = sb("w1_hi", [P, ALL, HID], F32R)
        w1_lo = sb("w1_lo", [P, ALL, HID], F32R)
        w2 = sb("w2", [P, ALL, HT, P])
        b1T = sb("b1T", [P, ALL, HT])
        b2_sb = sb("b2_sb", [E, P])
        sb2_all = sb("sb2_all", [P, S, P])
        rw_sb = sb("rw_sb", [P, E])
        rb_all = sb("rb_all", [P, E])
        hbuf = sb("hbuf", [P, 2 * HT, BANK])
        b1_rows = hbuf[0:ALL * HT, 2 * HT - 1, 0:P]
        stat = sb("stat", [P, 6, TILES])
        gate = sb("gate", [P, 7, TILES, E])
        rev = sb("rev", [P, E])
        wT = latT[0:E, :]
        minus_half = sb("minus_half", [P, TILES])
        ident = sb("ident", [P, P])
        ident_b = sb("ident_b", [P, P], BF16)
        mask_qk = sb("mask_qk", [P, P], BF16)
        mask_kq = sb("mask_kq", [P, P], BF16)
        wdown = sb("wdown", [P, P])
        wpair = sb("wpair", [P, 3, P])
        wo_sum = {h: sb(f"wo_sum_{h}", [DH + 1, C + 1]) for h in "AB"}
        q_both = {"A": xnT_hi, "B": sb("q_both_B", [P, T], F32R)}
        q_hi_m = {h: sb(f"q_hi_m_{h}", [DH + 2, T], F32R) for h in "AB"}
        k_hi2 = {"A": xnT_lo, "B": sb("k_hi2_B", [P, T], F32R)}
        k_lo_1 = {h: sb(f"k_lo_1_{h}", [DH + 2, T], F32R) for h in "AB"}
        v_one = {h: sb(f"v_one_{h}", [P, TILES, DH + 1]) for h in "AB"}
        v_stage = hbuf[:, 6:8, :].rearrange("p a (b d) -> p (a b) d", d=DH)
        prob = hbuf[:, 0:4, :]
        oT = hbuf[0:DH + 1, 4:6, :]
        max_part = sb("max_part", [P, TILES, GROUPS])
        max_q = sb("max_q", [P, TILES])
        max_hi = sb("max_hi", [TILES, P], F32R)
        max_lo = sb("max_lo", [TILES, P], F32R)
        recip = sb("recip", [P, 2, RT])
        HALF = {"A": (0, DH), "B": (DH, P)}
        OTHER = {"A": (DH, P), "B": (0, DH)}

        def w1_raw(e):
            if e < 2 * T // HID:
                return qk_stage[:].rearrange("p a t -> p (a t)")[:, e * HID:(e + 1) * HID]
            e -= 2 * T // HID
            return w1_rest[:].rearrange("p a t -> p (a t)")[:, e * HID:(e + 1) * HID]

        def max_bank(h, use):
            return bank[4 + ("AB".index(h) * MU + use) % 2]

        x_loaded, small_loaded, out_stored = sem("x_loaded"), sem("small_loaded"), sem("out_stored")
        w1_loaded = sem("w1_loaded")
        w2_loaded = sem("w2_loaded")
        pool_passed = sem("pool_passed")
        pool_step, consts_ready = sem("pool_step"), sem("consts_ready")
        dve_step = sem("dve_step")
        var_ready, rstd_ready, xn_ready = sem("var_ready"), sem("rstd_ready"), sem("xn_ready")
        xnT_mm, xnT_copied, xnT_split = sem("xnT_mm"), sem("xnT_copied"), sem("xnT_split")
        w1_hi_ready, w1_lo_ready = sem("w1_hi_ready"), sem("w1_lo_ready")
        gate_mm, gap_ready, gap_exp = sem("gate_mm"), sem("gap_ready"), sem("gap_exp")
        gate_ready, wT_mm, wT_copied, bias_mm = sem("gate_ready"), sem("wT_mm"), sem("wT_copied"), sem("bias_mm")
        b1_mm, b1T_ready = sem("b1_mm"), sem("b1T_ready")
        bias_read, rows_split, recip_done = (
            sem("bias_read"), sem("rows_split"), sem("recip_done"))
        h_mm, gelu_done, y_mm, y_added = sem("h_mm"), sem("gelu_done"), sem("y_mm"), sem("y_added")
        lat_mm, lat_copied = sem("lat_mm"), sem("lat_copied")
        wpair_loaded = sem("wpair_loaded")
        wo_loaded = {h: sem(f"wo_loaded_{h}") for h in "AB"}
        proj_mm, staged = sem("proj_mm"), sem("staged")
        hi_ready, v_ready, lo_ready, dup_loaded = sem("hi_ready"), sem("v_ready"), sem("lo_ready"), sem("dup_loaded")
        mx_mm, mx_read, max_ready = sem("mx_mm"), sem("mx_read"), sem("max_ready")
        rows_ready, rows_loaded = sem("rows_ready"), sem("rows_loaded")
        st_mm, exp_done, pv_mm, oT_copied = sem("st_mm"), sem("exp_done"), sem("pv_mm"), sem("oT_copied")
        op_mm, op_added = sem("op_mm"), sem("op_added")

        CR_GELU, CR_Y, CR_YA = HT, 2, 2
        CR_ST, CR_PV, CR_O, CR_MX, CR_OP = 2, 4, 2, 2, 1
        UNITS = 2 * GROUPS

        resid_flat = resid[:].rearrange("p a c -> p (a c)")
        x_tok = x.rearrange("o (a p) c -> p (o a) c", p=P)
        out_tok = out.rearrange("o (a p) c -> p (o a) c", p=P)
        block = ctx.enter_context(nc.Block())

        @block.sync
        def _(sp):
            sp.dma_start(resid[:], x_tok).then_inc(x_loaded, 16)
            sp.dma_start(rw_sb[:], rW).then_inc(small_loaded, 16)
            sp.dma_start(rb_all[:], rb.rearrange("(a e) -> a e", a=1).broadcast_to([P, E])).then_inc(small_loaded, 16)
            sp.dma_start(b1_rows[0:E * HT, :], b1.rearrange("e (h p) -> (e h) p", p=P)).then_inc(small_loaded, 16)
            sp.dma_start(b1_rows[E * HT:ALL * HT, :], sb1.rearrange("e (h p) -> (e h) p", p=P)).then_inc(small_loaded, 16)
            for e in range(ALL):
                src = W1[e] if e < E else sW1[e - E]
                sp.dma_start(w1_raw(e), src).then_inc(w1_loaded, 16)
            for s in range(S):
                sp.dma_start(sb2_all[:, s, :], sb2[s:s + 1, :].broadcast_to([P, P])).then_inc(small_loaded, 16)
            sp.dma_start(b2_sb[:], b2).then_inc(small_loaded, 16)
            sp.dma_start(wdown[:], w_kv_down).then_inc(small_loaded, 16)
            for e in range(ALL):
                src = W2[e] if e < E else sW2[e - E]
                sp.dma_start(w2[:, e, :, :], src.rearrange("(h p) d -> p h d", p=P)).then_inc(w2_loaded, 16)

            def load_wpair(pair):
                at = pair * P
                sp.dma_start(wpair[:, 1, :], w_q[:, bass.ds(at, P)]).then_inc(wpair_loaded, 16)
                sp.dma_start(wpair[:, 0, :], w_kv_up[:, bass.ds(at, P)]).then_inc(wpair_loaded, 16)
                sp.dma_start(wpair[:, 2, :], w_kv_up[:, bass.ds(at + HD, P)]).then_inc(wpair_loaded, 16)

            def duplicate(h, n):
                lo, hi = HALF[h]
                o_lo, o_hi = OTHER[h]
                sp.wait_ge(hi_ready, PIECES * n + PIECES)
                sp.dma_start(k_hi2[h][o_lo:o_hi, :].bitcast(F32), k_hi2[h][lo:hi, :].bitcast(F32)).then_inc(dup_loaded, 16)
                sp.dma_start(q_hi_m[h][0:DH, :].bitcast(F32), q_both[h][lo:hi, :].bitcast(F32)).then_inc(dup_loaded, 16)

            def max_rows(h, n):
                sp.wait_ge(rows_ready, n + 1)
                sp.dma_start(q_hi_m[h][DH:DH + 1, :].bitcast(F32), max_hi[:].bitcast(F32)).then_inc(rows_loaded, 16)
                sp.dma_start(q_hi_m[h][DH + 1:DH + 2, :].bitcast(F32), max_lo[:].bitcast(F32)).then_inc(rows_loaded, 16)

            load_wpair(0)
            duplicate("A", 0)
            max_rows("A", 0)

            def load_wo(h, p):
                row = (2 * p + "AB".index(h)) * DH
                sp.dma_start(wo_sum[h][0:DH, 0:C], w_out[bass.ds(row, DH), :]).then_inc(wo_loaded[h], 16)

            def pair_body(p, first=False, last=False):
                if first:
                    sp.wait_ge(consts_ready, 1)
                else:
                    sp.wait_ge(op_mm, ROUNDS * (UNITS * p - GROUPS))
                load_wo("A", p)
                if not first:
                    sp.wait_ge(op_mm, ROUNDS * UNITS * p)
                load_wo("B", p)
                if not last:
                    sp.wait_ge(proj_mm, PROJ * p + PROJ)
                    load_wpair(p + 1)
                duplicate("B", 2 * p + 1)
                max_rows("B", 2 * p + 1)
                if not last:
                    duplicate("A", 2 * p + 2)
                    max_rows("A", 2 * p + 2)

            pair_body(0, first=True)
            with sp.Fori(1, PAIRS - 1) as p:
                pair_body(p)
            pair_body(PAIRS - 1, last=True)

            sp.wait_ge(y_added, CR_YA + 2 * GROUPS * ALL)
            sp.dma_start(out_tok, resid[:]).then_inc(out_stored, 16)
            sp.wait_ge(out_stored, 16)

        @block.gpsimd
        def _(pool):
            pool.memset(ident[:], 0.0).then_inc(pool_step, 1)
            pool.memset(mask_qk[:], 0.0).then_inc(pool_step, 1)
            pool.memset(mask_kq[:], 0.0).then_inc(pool_step, 1)
            pool.memset(minus_half[:], -0.5).then_inc(pool_step, 1)
            pool.wait_ge(pool_step, 4)
            pool.affine_select(out=ident[:], in_=ident[:], compare_op=ALU.not_equal, fill=1.0, base=0,
                               pattern=[[-1, P]], channel_multiplier=1).then_inc(pool_step, 1)
            pool.affine_select(out=mask_qk[:], in_=mask_qk[:], compare_op=ALU.is_ge, fill=NEG, base=0,
                               pattern=[[-1, P]], channel_multiplier=1).then_inc(pool_step, 1)
            pool.affine_select(out=mask_kq[:], in_=mask_kq[:], compare_op=ALU.is_ge, fill=NEG, base=0,
                               pattern=[[1, P]], channel_multiplier=-1).then_inc(pool_step, 1)
            pool.wait_ge(pool_step, 7)
            for h in "AB":
                pool.memset(k_lo_1[h][DH:DH + 2, :].bitcast(F32), -1.0).then_inc(pool_step, 1)
                pool.wait_ge(pool_step, 8 + 3 * "AB".index(h))
                pool.memset(v_one[h][:, :, DH:DH + 1], 1.0).then_inc(pool_step, 1)
                pool.wait_ge(pool_step, 9 + 3 * "AB".index(h))
                pool.memset(wo_sum[h][:], 0.0).then_inc(pool_step, 1)
                pool.wait_ge(pool_step, 10 + 3 * "AB".index(h))
            pool.wait_ge(pool_step, 13)
            for h in "AB":
                pool.memset(wo_sum[h][DH:DH + 1, C:C + 1], 1.0).then_inc(pool_step, 1)
            pool.wait_ge(pool_step, 15)
            for e in range(E):
                pool.memset(rev[:, e:e + 1], float(E - e)).then_inc(pool_step, 1)
            pool.wait_ge(pool_step, 15 + E)
            pool.tensor_copy(ident_b[:], ident[:]).then_inc(consts_ready, 1)

            def rstd(norm):
                pool.wait_ge(var_ready, norm + 1)
                pool.tensor_tensor(stat[:, 4, :], stat[:, 3, :], minus_half[:], ALU.pow).then_inc(rstd_ready, 1)

            rstd(0)
            rstd(1)

            def pair_body(p):
                pool.wait_ge(st_mm, 2 * NS * p + 1)
                pool.wait_ge(pv_mm, 2 * NS * p + CR_PV)
                pool.wait_ge(staged, PROJ * p + PROJ)
                pool.sem_inc(pool_passed, 1)
                pool.tensor_copy(v_one["B"][:, :, 0:DH], v_stage).then_inc(v_ready, 1)
                pool.wait_ge(v_ready, p + 1)
                pool.sem_inc(pool_passed, 1)

            with pool.Fori(0, PAIRS) as p:
                pair_body(p)
            rstd(2)

        @block.scalar
        def _(act):
            act.sem_inc(gelu_done, CR_GELU)
            act.sem_inc(exp_done, CR_ST)
            act.sem_inc(oT_copied, CR_O)

            def copy_xnT(norm):
                for g in range(GROUPS):
                    act.wait_ge(xnT_mm, GROUPS * norm + g + 1)
                    act.activation(xnT[:, g * BANK:(g + 1) * BANK], bank[g][:], ACT.Copy).then_inc(xnT_copied, 1)

            def ffn(f):
                copy_xnT(2 * f)
                if f == 0:
                    for e in range(ALL):
                        act.wait_ge(w1_loaded, 16 * ALL)
                        act.activation(w1_hi[:, e, :], w1_raw(e), ACT.Copy).then_inc(w1_hi_ready, 1)
                act.wait_ge(gap_ready, f + 1)
                act.activation(gate[:, 4, :, 0], stat[:, 0, :], ACT.Exp).then_inc(gap_exp, 1)
                for g in range(GROUPS):
                    act.wait_ge(wT_mm, GROUPS * f + g + 1)
                    act.activation(wT[:, g * BANK:(g + 1) * BANK], bank[g][0:E, :], ACT.Copy).then_inc(wT_copied, 1)
                act.wait_ge(b1T_ready, 1)
                with act.Fori(0, GROUPS) as g:
                    for e in range(ALL):
                        y_at = (f * GROUPS + g) * ALL + e
                        act.wait_ge(y_mm, y_at - 2 + 1 + CR_Y)
                        for ht in range(HT):
                            act.wait_ge(h_mm, y_at * HT + ht + 1)
                            act.activation(hbuf[:, e % 2 * HT + ht, :], bank[ht][:], ACT.Gelu,
                                           bias=b1T[:, e, ht:ht + 1]).then_inc(gelu_done, 1)

            ffn(0)

            copy_xnT(1)
            for g in range(GROUPS):
                act.wait_ge(lat_mm, g + 1)
                act.activation(latT[:, g * BANK:(g + 1) * BANK], bank[4 + g][:], ACT.Copy).then_inc(lat_copied, 1)

            def round_piece(h, m, src):
                lo, hi = HALF[h]
                dst = (k_hi2, q_both)[m % 2][h]
                act.activation(dst[lo:hi, m // 2 * BANK:(m // 2 + 1) * BANK], src, ACT.Copy).then_inc(hi_ready, 1)

            def stage(pair, k):
                act.wait_ge(proj_mm, PROJ * pair + k + 1)
                if k < PIECES:
                    lo, hi = HALF["A"]
                    round_piece("A", k, bank[6][lo:hi, :])
                    act.activation(qk_stage[:, k % 2, k // 2 * BANK:(k // 2 + 1) * BANK], bank[6][:], ACT.Copy)\
                       .then_inc(staged, 1)
                else:
                    tiles = slice(GQ * (k - PIECES), GQ * (k - PIECES) + GQ)
                    v = bank[6][:].rearrange("p (a d) -> p a d", a=GQ)
                    act.activation(v_one["A"][:, tiles, 0:DH], v[:, :, 0:DH], ACT.Copy)
                    act.activation(v_stage[:, tiles, :], v[:, :, DH:P], ACT.Copy).then_inc(staged, 1)

            for k in range(PROJ):
                stage(0, k)

            def copy_oT(p, u, first=False):
                unit = UNITS * p + u
                last_step = NS * (u // GROUPS) + UNIT_LAST[u % GROUPS]
                act.wait_ge(pv_mm, 2 * NS * p + last_step + 1 + CR_PV)
                if not (first and u < 2):
                    act.wait_ge(op_mm, ROUNDS * (unit - 1))
                act.activation(oT[:, u % 2, :], bank[2 + u % 2][0:DH + 1, :], ACT.Copy).then_inc(oT_copied, 1)

            def pair_body(p, first=False, last=False):
                for n in range(2 * NS):
                    s, head = n % NS, n // NS
                    g, j = STEPS[s]
                    at = max(GQ * g, j)
                    width = (GQ * g + GQ - at) * P
                    act.wait_ge(st_mm, 2 * NS * p + n + 1)
                    act.wait_ge(pv_mm, 2 * NS * p + n + 1)
                    act.activation(prob[:, n % 4, 0:width], bank[n % 2][:, 0:width], ACT.Exp, scale=SCALE)\
                       .then_inc(exp_done, 1)
                    u = unit_ended(n - COPY_LAG)
                    if u is not None and not (first and u < 0):
                        copy_oT(p, u, first)
                    if head == 0 and s < len(PIECE_SLOTS["A"]):
                        for m in PIECE_SLOTS["A"][s]:
                            lo, hi = HALF["B"]
                            round_piece("B", m, qk_stage[lo:hi, m % 2, m // 2 * BANK:(m // 2 + 1) * BANK])
                    if head == 1 and s < PROJ and not last:
                        if s == 0:
                            act.wait_ge(lo_ready, PIECES * (2 * p + 2))
                        if s == PIECES:
                            act.wait_ge(v_ready, p + 1)
                        stage(p + 1, s)

            pair_body(0, first=True)
            with act.Fori(1, PAIRS - 1) as p:
                pair_body(p)
            pair_body(PAIRS - 1, last=True)
            copy_oT(PAIRS, -1)
            ffn(1)

        @block.vector
        def _(dve):
            step = [0]

            def link(ins):
                step[0] += 1
                ins.then_inc(dve_step, 1)
                dve.wait_ge(dve_step, step[0])

            def over_channels(ap):
                return ap.rearrange("p (a o) -> p a o", o=1).broadcast_to([P, TILES, P])

            def over_experts(ap):
                return ap.rearrange("p (a o) -> p a o", o=1).broadcast_to([P, TILES, E])

            def norm(n):
                link(dve.reduce_sum(stat[:, 1, :], resid[:], axis=AX.X))
                link(dve.tensor_scalar(stat[:, 2, :], stat[:, 1, :], 1.0 / C, None, ALU.mult))
                link(dve.tensor_tensor(xn[:], resid[:], over_channels(stat[:, 2, :]), ALU.subtract))
                square = xnT[:].rearrange("p (a c) -> p a c", c=P)
                link(dve.tensor_tensor(square, xn[:], xn[:], ALU.mult))
                link(dve.reduce_sum(stat[:, 1, :], square, axis=AX.X))
                dve.tensor_scalar(stat[:, 3, :], stat[:, 1, :], 1.0 / C, EPS, ALU.mult, ALU.add).then_inc(var_ready, 1)
                dve.wait_ge(rstd_ready, n + 1)
                dve.tensor_tensor(xn[:], xn[:], over_channels(stat[:, 4, :]), ALU.mult).then_inc(xn_ready, 1)

            def split_xnT(n):
                dve.wait_ge(xnT_copied, GROUPS * (n + 1))
                link(dve.tensor_copy(xnT_hi[:], xnT[:]))
                dve.tensor_tensor(xnT_lo[:], xnT[:], xnT_hi[:].bitcast(F32), ALU.subtract).then_inc(xnT_split, 1)

            def ffn(f):
                norm(2 * f)
                split_xnT(2 * f)
                if f == 0:
                    for e in range(ALL):
                        dve.wait_ge(w1_hi_ready, e + 1)
                        dve.tensor_tensor(w1_lo[:, e, :], w1_raw(e), w1_hi[:, e, :].bitcast(F32), ALU.subtract)\
                           .then_inc(w1_lo_ready, 1)
                G, EQ, KEY, OH1, G2, OH2, W = range(7)
                dve.wait_ge(gate_mm, f + 1)
                gates = bank[4][:, 0:TILES * E].rearrange("p (a e) -> p a e", e=E)
                rb_b = rb_all[:].rearrange("p (o e) -> p o e", o=1).broadcast_to([P, TILES, E])
                rev_b = rev[:].rearrange("p (o e) -> p o e", o=1).broadcast_to([P, TILES, E])
                link(dve.tensor_tensor(gate[:, G], gates, rb_b, ALU.add))
                for src, best, onehot in ((G, 1, OH1), (G2, 2, OH2)):
                    if src == G2:
                        link(dve.scalar_tensor_tensor(out=gate[:, G2], in0=gate[:, OH1], scalar=-BIG,
                                                      in1=gate[:, G], op0=ALU.mult, op1=ALU.add))
                    link(dve.reduce_max(stat[:, best, :], gate[:, src], axis=AX.X))
                    link(dve.tensor_tensor(gate[:, EQ], gate[:, src], over_experts(stat[:, best, :]), ALU.is_equal))
                    link(dve.tensor_tensor(gate[:, KEY], gate[:, EQ], rev_b, ALU.mult))
                    link(dve.reduce_max(stat[:, 5, :], gate[:, KEY], axis=AX.X))
                    link(dve.tensor_tensor(gate[:, onehot], gate[:, KEY], over_experts(stat[:, 5, :]), ALU.is_equal))
                dve.tensor_tensor(stat[:, 0, :], stat[:, 2, :], stat[:, 1, :], ALU.subtract).then_inc(gap_ready, 1)
                dve.wait_ge(gap_exp, f + 1)
                ex = gate[:, G2, :, 0]
                link(dve.tensor_scalar(stat[:, 3, :], ex, 1.0, None, ALU.add))
                link(dve.reciprocal(stat[:, 5, :], stat[:, 3, :]))
                link(dve.tensor_scalar(stat[:, 1, :], stat[:, 5, :], 0.5, None, ALU.mult))
                link(dve.tensor_tensor(stat[:, 2, :], ex, stat[:, 1, :], ALU.mult))
                link(dve.tensor_tensor(gate[:, EQ], gate[:, OH1], over_experts(stat[:, 1, :]), ALU.mult))
                link(dve.tensor_tensor(gate[:, KEY], gate[:, OH2], over_experts(stat[:, 2, :]), ALU.mult))
                dve.tensor_tensor(gate[:, W], gate[:, EQ], gate[:, KEY], ALU.add).then_inc(gate_ready, 1)
                if f == 0:
                    dve.wait_ge(b1_mm, 1)
                    dve.tensor_copy(b1T[:].rearrange("p e h -> p (e h)"), bank[5][:, 0:ALL * HT]).then_inc(b1T_ready, 1)
                    dve.wait_ge(small_loaded, 16 * (6 + S))
                    link(dve.tensor_tensor(sb2_all[:, 0, :], sb2_all[:, 0, :], sb2_all[:, 1, :], ALU.add))
                shared = sb2_all[:, 0:1, :].broadcast_to([P, TILES, P])
                link(dve.scalar_tensor_tensor(out=resid[:], in0=shared, scalar=0.5 / S, in1=resid[:],
                                              op0=ALU.mult, op1=ALU.add))
                for g in range(GROUPS):
                    dve.wait_ge(bias_mm, GROUPS * f + g + 1)
                    part = resid_flat[:, g * BANK:(g + 1) * BANK]
                    dve.tensor_tensor(part, bank[6 + g % 2][:], part, ALU.add).then_inc(bias_read, 1)
                dve.wait_ge(bias_read, GROUPS * (f + 1))
                dve.wait_ge(gate_ready, f + 1)
                with dve.Fori(0, GROUPS) as g:
                    for e in range(ALL):
                        y_at = (f * GROUPS + g) * ALL + e
                        dve.wait_ge(y_mm, y_at + 1 + CR_Y)
                        dve.wait_ge(y_added, y_at + CR_YA)
                        for t in range(GQ):
                            part = resid[:, bass.ds(g * GQ + t, 1), :].rearrange("p o c -> p (o c)")
                            weight = 0.5 / S if e >= E else \
                                gate[:, W, bass.ds(g * GQ + t, 1), e:e + 1].rearrange("p o e -> p (o e)")
                            ins = dve.scalar_tensor_tensor(
                                out=part, in0=bank[6 + e % 2][:, t * P:(t + 1) * P], scalar=weight, in1=part,
                                op0=ALU.mult, op1=ALU.add)
                        ins.then_inc(y_added, 1)
                dve.wait_ge(y_added, (f + 1) * GROUPS * ALL + CR_YA)

            dve.sem_inc(y_added, CR_YA)
            dve.sem_inc(mx_read, CR_MX)
            dve.sem_inc(op_added, CR_OP)
            dve.wait_ge(x_loaded, 16)
            dve.wait_ge(consts_ready, 1)
            ffn(0)
            norm(1)
            link(dve.memset(max_part[:], -BIG))

            def split_lo(h, n, m, pair):
                lo, hi = HALF[h]
                o_lo, o_hi = (0, DH) if m % 2 == 0 else OTHER[h]
                dst, rounded = ((k_lo_1, k_hi2), (q_both, q_both))[m % 2]
                cols = slice(m // 2 * BANK, (m // 2 + 1) * BANK)
                dve.wait_ge(staged, PROJ * pair + m + 1)
                dve.wait_ge(hi_ready, PIECES * n + m + 1)
                dve.tensor_tensor(dst[h][o_lo:o_hi, cols], qk_stage[lo:hi, m % 2, cols],
                                  rounded[h][lo:hi, cols].bitcast(F32), ALU.subtract).then_inc(lo_ready, 1)

            def reduce_chunk(h, n, c):
                i, part = CHUNKS[c]
                width = min(BANK, (i + 1) * P - part * BANK)
                dve.wait_ge(mx_mm, MU * n + c + 1)
                dve.reduce_max(max_part[:, i, part:part + 1], max_bank(h, c)[:, 0:width], axis=AX.X)\
                   .then_inc(mx_read, 1)

            def reduce_last(n):
                dve.wait_ge(mx_read, MU * n + NC + CR_MX)
                dve.reduce_max(max_q[:], max_part[:], axis=AX.X).then_inc(max_ready, 1)

            def split_rows(h, n, first=False):
                src = max_bank(h, NC)[0:TILES, 0:P]
                dve.wait_ge(mx_mm, MU * n + NC + 1)
                if not first:
                    dve.wait_ge(rows_loaded, 32 * n)
                dve.tensor_copy(max_hi[:], src).then_inc(rows_split, 1)
                dve.wait_ge(rows_split, n + 1)
                dve.tensor_tensor(max_lo[:], src, max_hi[:].bitcast(F32), ALU.subtract).then_inc(mx_read, 1)
                dve.wait_ge(mx_read, MU * n + MU + CR_MX)
                dve.sem_inc(rows_ready, 1)

            def add_out(p, u, r):
                rounds = ROUNDS * (UNITS * p + u) + r
                dve.wait_ge(op_mm, rounds + 1)
                dve.wait_ge(op_added, rounds + CR_OP)
                o = bank[7][:, 0:RT * (C + 1)].rearrange("p (a d) -> p a d", d=C + 1)
                dve.reciprocal(recip[:, r % 2, :], o[:, :, C]).then_inc(recip_done, 1)
                dve.wait_ge(recip_done, rounds + 1)
                for t in range(RT):
                    part = resid[:, u % GROUPS * GQ + r * RT + t, :]
                    ins = dve.scalar_tensor_tensor(out=part, in0=o[:, t, 0:C], scalar=recip[:, r % 2, t:t + 1],
                                                   in1=part, op0=ALU.mult, op1=ALU.add)
                ins.then_inc(op_added, 1)

            for m in range(PIECES):
                split_lo("A", 0, m, 0)
            for c in range(NC):
                reduce_chunk("A", 0, c)
            reduce_last(0)
            split_rows("A", 0, first=True)

            def pair_body(p, first=False, last=False):
                for n in range(2 * NS):
                    s, head = n % NS, n // NS
                    here, nxt = "AB"[head], "BA"[head]
                    number = 2 * p + 1 + head
                    if not (last and head == 1):
                        if s < len(PIECE_SLOTS[here]):
                            for m in PIECE_SLOTS[here][s]:
                                split_lo(nxt, number, m, p + head)
                        for c in range(2 * (s - CHUNK_FROM[here]), 2 * (s - CHUNK_FROM[here]) + 2):
                            if 0 <= c < NC:
                                reduce_chunk(nxt, number, c)
                        if s == MAX_SLOT[here]:
                            reduce_last(number)
                        if s == ROW_SLOT[here]:
                            split_rows(nxt, number)
                    for r in range(ROUNDS):
                        u = unit_ended(n - COPY_LAG - 1 - r)
                        if u is not None and not (first and u < 0):
                            add_out(p, u, r)

            pair_body(0, first=True)
            with dve.Fori(1, PAIRS - 1) as p:
                pair_body(p)
            pair_body(PAIRS - 1, last=True)
            for r in range(ROUNDS):
                add_out(PAIRS, -1, r)
            dve.wait_ge(op_added, ROUNDS * UNITS * PAIRS + CR_OP)
            ffn(1)

        @block.tensor
        def _(pe):
            pe.sem_inc(y_mm, CR_Y)
            pe.sem_inc(pv_mm, CR_PV)

            def three_pass(dst, l_hi, l_lo, r_hi, r_lo):
                pe.matmul(dst, l_hi, r_hi, start=True, stop=False)
                pe.matmul(dst, l_hi, r_lo, start=False, stop=False)
                return pe.matmul(dst, l_lo, r_hi, start=False, stop=True)

            def transpose_xn(n):
                pe.wait_ge(xn_ready, n + 1)
                for g in range(GROUPS):
                    for t in range(GQ):
                        ins = pe.transpose(bank[g][:, t * P:(t + 1) * P], xn[:, g * GQ + t, :], ident[:])
                    ins.then_inc(xnT_mm, 1)

            def ffn(f):
                transpose_xn(2 * f)
                pe.wait_ge(xnT_copied, GROUPS * (2 * f + 1))
                if f == 0:
                    pe.wait_ge(small_loaded, 16 * (6 + S))
                    pe.transpose(bank[5][:, 0:ALL * HT], b1_rows, ident[0:ALL * HT, 0:ALL * HT]).then_inc(b1_mm, 1)
                for t in range(TILES):
                    ins = pe.matmul(bank[4][:, t * E:(t + 1) * E], xnT[:, t * P:(t + 1) * P], rw_sb[:],
                                    start=True, stop=True)
                ins.then_inc(gate_mm, 1)
                pe.wait_ge(gate_ready, f + 1)
                for g in range(GROUPS):
                    for t in range(GQ):
                        ins = pe.transpose(bank[g][0:E, t * P:(t + 1) * P], gate[:, 6, g * GQ + t, :], ident[:])
                    ins.then_inc(wT_mm, 1)
                pe.wait_ge(wT_copied, GROUPS * (f + 1))
                for g in range(GROUPS):
                    if g >= 2:
                        pe.wait_ge(bias_read, GROUPS * f + g - 1)
                    for t in range(GQ):
                        tile = g * GQ + t
                        ins = pe.matmul(bank[6 + g % 2][:, t * P:(t + 1) * P], wT[:, tile * P:(tile + 1) * P],
                                        b2_sb[:], start=True, stop=True)
                    ins.then_inc(bias_mm, 1)
                pe.wait_ge(bias_read, GROUPS * (f + 1))
                pe.wait_ge(xnT_split, f + 1)
                if f == 0:
                    pe.wait_ge(w1_lo_ready, ALL)
                    pe.wait_ge(w2_loaded, 16 * ALL)

                def second_layer(g, e):
                    y_at = (f * GROUPS + g) * ALL + e
                    pe.wait_ge(gelu_done, y_at * HT + HT + CR_GELU)
                    pe.wait_ge(y_added, y_at - 2 + 1 + CR_YA)
                    for t in range(GQ):
                        for ht in range(HT):
                            ins = pe.matmul(bank[6 + e % 2][:, t * P:(t + 1) * P],
                                            hbuf[:, e % 2 * HT + ht, t * P:(t + 1) * P], w2[:, e, ht, :],
                                            start=ht == 0, stop=ht == HT - 1)
                    ins.then_inc(y_mm, 1)

                with pe.Fori(0, GROUPS) as g:
                    x_hi = xnT_hi[:, bass.ds(g * BANK, BANK)]
                    x_lo = xnT_lo[:, bass.ds(g * BANK, BANK)]
                    for e in range(ALL):
                        for ht in range(HT):
                            at = ((f * GROUPS + g) * ALL + e) * HT + ht
                            pe.wait_ge(gelu_done, at - HT + 1 + CR_GELU)
                            cols = slice(ht * P, (ht + 1) * P)
                            three_pass(bank[ht][:], w1_hi[:, e, cols], w1_lo[:, e, cols], x_hi, x_lo)\
                                .then_inc(h_mm, 1)
                        if e >= 1:
                            second_layer(g, e - 1)
                    second_layer(g, ALL - 1)

            pe.wait_ge(consts_ready, 1)
            ffn(0)

            transpose_xn(1)
            pe.wait_ge(xnT_copied, 2 * GROUPS)
            pe.wait_ge(y_added, GROUPS * ALL + CR_YA)
            for g in range(GROUPS):
                pe.matmul(bank[4 + g][:], wdown[:], xnT[:, g * BANK:(g + 1) * BANK], start=True, stop=True)\
                  .then_inc(lat_mm, 1)
            pe.wait_ge(lat_copied, GROUPS)

            def project(pair, k):
                if k == 0:
                    pe.wait_ge(wpair_loaded, 48 * pair + 48)
                if not (k == 0 and isinstance(pair, int) and pair == 0):
                    pe.wait_ge(staged, PROJ * pair + k)
                if k < PIECES:
                    src = latT if k % 2 == 0 else xnT
                    pe.matmul(bank[6][:], wpair[:, k % 2, :], src[:, k // 2 * BANK:(k // 2 + 1) * BANK],
                              start=True, stop=True).then_inc(proj_mm, 1)
                else:
                    for t in range(GQ):
                        tile = GQ * (k - PIECES) + t
                        ins = pe.matmul(bank[6][:, t * P:(t + 1) * P], latT[:, tile * P:(tile + 1) * P],
                                        wpair[:, 2, :], start=True, stop=True)
                    ins.then_inc(proj_mm, 1)

            def max_chunk(h, n, c):
                i, part = CHUNKS[c]
                lo, hi = HALF[h]
                width = min(BANK, (i + 1) * P - part * BANK)
                diagonal = part == i // GQ
                dst = max_bank(h, c)
                pe.wait_ge(mx_read, MU * n + c - 2 + 1 + CR_MX)
                ins = pe.matmul(dst[:, 0:width], q_both[h][lo:hi, i * P:(i + 1) * P],
                                k_hi2[h][lo:hi, part * BANK:part * BANK + width], start=True, stop=not diagonal)
                if diagonal:
                    ins = pe.matmul(dst[:, width - P:width], ident_b[:], mask_qk[:], start=False, stop=True)
                ins.then_inc(mx_mm, 1)

            def max_transpose(h, n):
                pe.wait_ge(max_ready, n + 1)
                pe.wait_ge(mx_read, MU * n + NC - 2 + 1 + CR_MX)
                pe.transpose(max_bank(h, NC)[0:TILES, 0:P], max_q[:], ident[:]).then_inc(mx_mm, 1)

            for k in range(PROJ):
                project(0, k)
            pe.wait_ge(hi_ready, PIECES)
            for c in range(NC):
                max_chunk("A", 0, c)
            max_transpose("A", 0)

            def scores(p, n):
                head, s = n // NS, n % NS
                h = "AB"[head]
                g, j = STEPS[s]
                at = max(GQ * g, j)
                width = (GQ * g + GQ - at) * P
                keys, queries = slice(j * P, (j + 1) * P), slice(at * P, at * P + width)
                diagonal = j >= GQ * g
                dst = bank[n % 2]
                if s == 0:
                    number = 2 * p + head
                    pe.wait_ge(lo_ready, PIECES * (number + 1))
                    pe.wait_ge(dup_loaded, 32 * number + 32)
                    pe.wait_ge(rows_loaded, 32 * number + 32)
                pe.wait_ge(exp_done, 2 * NS * p + n - 2 + 1 + CR_ST)
                pe.matmul(dst[:, 0:width], k_hi2[h][:, keys], q_both[h][:, queries], start=True, stop=False)
                ins = pe.matmul(dst[:, 0:width], k_lo_1[h][:, keys], q_hi_m[h][:, queries],
                                start=False, stop=not diagonal)
                if diagonal:
                    ins = pe.matmul(dst[:, 0:P], ident_b[:], mask_kq[:], start=False, stop=True)
                ins.then_inc(st_mm, 1)

            def weigh(p, n):
                head, s = n // NS, n % NS
                g, j = STEPS[s]
                at = max(GQ * g, j)
                u = GROUPS * head + g
                if j == 0:
                    pe.wait_ge(oT_copied, UNITS * p + u - 2 + 1 + CR_O)
                if s == 0:
                    if head % 2 == 1:
                        pe.wait_ge(v_ready, p + 1)
                    else:
                        pe.wait_ge(staged, PROJ * p + PROJ)
                pe.wait_ge(exp_done, 2 * NS * p + n + 1 + CR_ST)
                pe.matmul(bank[2 + u % 2][0:DH + 1, (at - GQ * g) * P:BANK], v_one["AB"[head % 2]][:, j, :],
                          prob[:, n % 4, 0:(GQ * g + GQ - at) * P],
                          start=j == 0, stop=j == GQ * g + GQ - 1).then_inc(pv_mm, 1)

            def out_project(p, u, r):
                unit = UNITS * p + u
                pe.wait_ge(oT_copied, unit + 1 + CR_O)
                pe.wait_ge(op_added, ROUNDS * unit + r + CR_OP)
                h = "AB"[u // GROUPS % 2]
                if u % GROUPS == 0:
                    pe.wait_ge(wo_loaded[h], 16 * p + 16)
                for t in range(RT):
                    cols = slice((r * RT + t) * P, (r * RT + t + 1) * P)
                    ins = pe.matmul(bank[7][:, t * (C + 1):(t + 1) * (C + 1)], oT[:, u % 2, cols], wo_sum[h][:],
                                    start=True, stop=True)
                ins.then_inc(op_mm, 1)

            def pair_body(p, first=False, last=False):
                for n in range(2 * NS):
                    s, head = n % NS, n // NS
                    here, nxt = "AB"[head], "BA"[head]
                    number = 2 * p + 1 + head
                    scores(p, n)
                    if not (last and head == 1):
                        if head == 1 and s < PROJ:
                            project(p + 1, s)
                        if s == CHUNK_FROM[here]:
                            pe.wait_ge(hi_ready, PIECES * (number + 1))
                        for c in range(2 * (s - CHUNK_FROM[here]), 2 * (s - CHUNK_FROM[here]) + 2):
                            if 0 <= c < NC:
                                max_chunk(nxt, number, c)
                        if s == ROW_SLOT[here]:
                            max_transpose(nxt, number)
                    if not (first and n == 0):
                        weigh(p, n - 1)
                    for r in range(ROUNDS):
                        u = unit_ended(n - COPY_LAG - 1 - r)
                        if u is not None and not (first and u < 0):
                            out_project(p, u, r)

            pair_body(0, first=True)
            with pe.Fori(1, PAIRS - 1) as p:
                pair_body(p)
            pair_body(PAIRS - 1, last=True)
            weigh(PAIRS, -1)
            for r in range(ROUNDS):
                out_project(PAIRS, -1, r)
            ffn(1)


_INS = ["L0_attn_x", "L0_attn_w_kv_down", "L0_attn_w_kv_up", "L0_attn_w_q", "L0_attn_w_out", "L0_ffn_rW",
        "L0_ffn_rb", "L0_ffn_W1", "L0_ffn_b1", "L0_ffn_W2", "L0_ffn_b2", "L0_ffn_sW1", "L0_ffn_sb1",
        "L0_ffn_sW2", "L0_ffn_sb2"]


def kernel(**inputs):
    import concourse.bacc as _bacc
    from concourse.bass_utils import run_bass_kernel_spmd as _run

    nc = _bacc.Bacc("TRN2", target_bir_lowering=False, num_devices=1)
    arrays, args = {}, []
    for name in _INS:
        a = np.ascontiguousarray(inputs[name])
        arrays[f"in_{name}"] = a
        args.append(nc.dram_tensor(f"in_{name}", a.shape, mybir.dt.from_np(a.dtype), kind="ExternalInput").ap())
    shape = inputs["L0_attn_x"].shape
    args.append(nc.dram_tensor("out_x", shape, F32, kind="ExternalOutput").ap())
    macaron_kernel(nc, *args)
    r = _run(nc, [arrays], core_ids=[0])
    return r.results[0]["out_x"]
```

```python
from contextlib import ExitStack

import numpy as np

import concourse.bass as bass
from concourse import mybir

F32 = mybir.dt.float32
F32R = mybir.dt.float32r
BF16 = mybir.dt.bfloat16
ALU = mybir.AluOpType
ACT = mybir.ActivationFunctionType
AX = mybir.AxisListType

P = 128
BANK = 512
NEG = -1.0e30
BIG = 3.0e38
EPS = 1e-5

GQ = BANK // P


def head_steps(tiles):
    return [(g, j) for g in range(tiles // GQ) for j in range(GQ * g + GQ)]


def max_chunks(tiles):
    return [(i, c) for i in range(tiles) for c in range(i // GQ + 1)]


def macaron_kernel(nc, x, w_kv_down, w_kv_up, w_q, w_out, rW, rb, W1, b1, W2, b2, sW1, sb1, sW2, sb2, out):
    T, C = x.shape[1], x.shape[2]
    TILES = T // P
    GROUPS = T // BANK
    HD = w_q.shape[1]
    DH = 64
    PAIRS = HD // (2 * DH)
    E, _, HID = W1.shape
    S = sW1.shape[0]
    ALL = E + S
    HT = HID // P
    SCALE = float(DH) ** -0.5
    STEPS = head_steps(TILES)
    NS = len(STEPS)
    CHUNKS = max_chunks(TILES)
    NC = len(CHUNKS)

    def chunks_of(g):
        return [c for c in range(NC) if CHUNKS[c][0] // GQ == g]

    MU = NC + 1
    assert C == P and TILES % GQ == 0 and NS % 4 == 0 and TILES * E == P
    UNIT_LAST = [STEPS.index((g, GQ * g + GQ - 1)) for g in range(GROUPS)]

    def unit_ended(n):
        head, s = n // NS, n % NS
        return GROUPS * head + UNIT_LAST.index(s) if s in UNIT_LAST else None

    PIECES = 2 * (T // BANK)
    PROJ = PIECES + T // BANK
    W1_AHEAD = 2
    WT_AT = [1, 2]
    SPLIT_LAG = 1
    V_SLOTS = [9, 11]
    V_STEPS = T // BANK + len(V_SLOTS)
    CHUNK_FROM = {"A": 3, "B": 3}
    MAX_SLOT = 35
    ROW_SLOT = MAX_SLOT + 1
    CHUNK_SLOTS = {h: [a + c * (MAX_SLOT - a) // NC for c in range(NC)] for h, a in CHUNK_FROM.items()}
    WEIGH_LAG, COPY_LAG, INVERT_LAG, NORM_LAG, PROJECT_LAG, RETURN_LAG = 2, 3, 6, 12, 14, 16

    with ExitStack() as ctx:
        def sb(name, shape, dt=F32):
            return ctx.enter_context(nc.sbuf_tensor(name, shape, dt))

        def sem(name):
            return ctx.enter_context(nc.semaphore(name))

        bank = [ctx.enter_context(nc.psum_tensor(f"bank{i}", [P, BANK], F32)) for i in range(8)]

        resid = sb("resid", [P, TILES, P])
        xn = sb("xn", [P, TILES, P])
        latT = xn[:].rearrange("p a c -> p (a c)")
        xnT = sb("xnT", [P, T])
        xnT_hi = sb("xnT_hi", [P, T], F32R)
        xnT_lo = sb("xnT_lo", [P, T], F32R)
        qk_stage = sb("qk_stage", [P, 2, T])
        w1_hi = sb("w1_hi", [P, ALL, HID], F32R)
        w1_lo = sb("w1_lo", [P, ALL, HID], F32R)
        w2_hi = sb("w2_hi", [P, ALL, HT, P], F32R)
        V1 = TILES * (DH + 1)
        W2_KEPT = ALL - 2 * V1 // HID
        w2_lo_kept = sb("w2_lo_kept", [P, W2_KEPT, HT, P], F32R)
        v_B = sb("v_B", [P, 2 * V1], F32R)
        b1T = sb("b1T", [P, ALL, HT])
        b2T = sb("b2T", [P, ALL])
        rw_sb = sb("rw_sb", [P, E])
        rb_all = sb("rb_all", [P, E])
        hbuf = sb("hbuf", [P, 2 * HT, BANK])
        b1_rows = hbuf[0:ALL * HT, 2 * HT - 1, 0:P]
        b2_rows = hbuf[0:ALL, 2 * HT - 2, 0:P]
        w_all = qk_stage[:].rearrange("p a (b c) -> p (a b) c", c=BANK)
        stat = sb("stat", [P, 6, TILES])
        bn = sb("bn", [P, TILES, 6])
        mean_var = sb("mean_var", [P, TILES, 2])
        gate = sb("gate", [P, 7, TILES, E])
        rev = sb("rev", [P, E])
        wT = latT[0:E, :]
        minus_half = sb("minus_half", [P, TILES])
        euler = sb("euler", [P, TILES])
        ident = sb("ident", [P, P])
        ident_b = sb("ident_b", [P, P], BF16)
        mask_qk = sb("mask_qk", [P, P], BF16)
        mask_kq = sb("mask_kq", [P, P], BF16)
        wdown = sb("wdown", [P, P])
        wpair = sb("wpair", [P, 3, P])
        wo_pair = sb("wo_pair", [P, C])
        q_hi_m_B, k_lo_1_B = sb("q_hi_m_B", [P, T], F32R), sb("k_lo_1_B", [P, T], F32R)
        q_both = {"A": xnT_hi, "B": sb("q_both_B", [P, T], F32R)}
        w1_hi_flat, w1_lo_flat = (w[:].rearrange("p e h -> p (e h)") for w in (w1_hi, w1_lo))
        q_hi_m = {"A": w1_hi_flat[0:DH + 2, 0:T],
                  "B": q_hi_m_B[0:DH + 2, :]}
        prob_hi = w1_hi_flat[:, T:2 * T].rearrange("p (r c) -> p r c", c=BANK)
        prob_lo = w1_hi_flat[:, 2 * T:2 * T + 2 * BANK].rearrange("p (r c) -> p r c", c=BANK)
        k_hi2 = {"A": xnT_lo, "B": sb("k_hi2_B", [P, T], F32R)}
        k_lo_1 = {"A": w1_lo_flat[0:DH + 2, 0:T],
                  "B": k_lo_1_B[0:DH + 2, :]}
        v_hi_one = {"A": w1_lo_flat[:, T:T + V1].rearrange("p (a d) -> p a d", d=DH + 1),
                    "B": v_B[:, 0:V1].rearrange("p (a d) -> p a d", d=DH + 1)}
        v_lo_0 = {"A": w1_lo_flat[:, T + V1:T + 2 * V1].rearrange("p (a d) -> p a d", d=DH + 1),
                  "B": v_B[:, V1:2 * V1].rearrange("p (a d) -> p a d", d=DH + 1)}
        v_stage = hbuf[:, 2:4, :].rearrange("p a (b d) -> p (a b) d", d=DH)
        prob = hbuf[:, 0:2, :]
        oT = hbuf[:, 4:4 + GROUPS, :]
        max_part = sb("max_part", [P, TILES, GROUPS])
        max_q = sb("max_q", [P, TILES])
        max_hi = sb("max_hi", [TILES, P], F32R)
        max_lo = sb("max_lo", [TILES, P], F32R)
        raw = sb("raw", [P, 2, BANK])
        sums = sb("sums", [DH, 2, BANK // DH])
        inv_sums = sb("inv_sums", [DH, 2, BANK // DH])
        inv_row = raw[96:97, :, :]
        inv_all = [w1_lo_flat[0:DH, ALL * HID - BANK:ALL * HID].bitcast(F32),
                   gate[:].rearrange("p a b c -> p (a b c)")[0:DH, 0:BANK]]
        product = raw
        yT = sb("yT", [P, T])
        HALF = {"A": (0, DH), "B": (DH, P)}
        OTHER = {"A": (DH, P), "B": (0, DH)}

        def w2_lo(e):
            if e < W2_KEPT:
                return w2_lo_kept[:, e, :, :]
            at = (e - W2_KEPT) * HID
            return v_B[:, at:at + HID].rearrange("p (h d) -> p h d", d=P)

        RING = 4

        def w1_raw(e):
            return w_all[:, RING + e % 2, :]

        def w2_raw(e):
            return w_all[:, RING + 2 + e % 2, :].rearrange("p (h d) -> p h d", d=P)

        def proj_bank(k):
            return bank[6 + k % 2]

        def max_ring(h, n):
            if isinstance(n, int) and n == 0:
                return (4, 5, 0, 1)
            return (4, 5) if h == "A" else (4, 5, 6)

        h_hi = [t[:].rearrange("p (a b) -> p a b", b=BANK) for t in (q_both["B"], k_hi2["B"])]
        h_lo = [t[:].rearrange("p (a b) -> p a b", b=BANK) for t in (q_hi_m_B, k_lo_1_B)]

        x_loaded = [sem(f"x_loaded_{g}") for g in range(GROUPS)]
        small_loaded, out_stored = sem("small_loaded"), sem("out_stored")
        w1_loaded = [sem(f"w1_loaded_{e}") for e in range(ALL)]
        w2_loaded = [sem(f"w2_loaded_{e}") for e in range(ALL)]
        pool_step, consts_ready = sem("pool_step"), sem("consts_ready")
        dve_step = sem("dve_step")
        var_ready, rstd_ready, xn_ready = sem("var_ready"), sem("rstd_ready"), sem("xn_ready")
        xnT_mm, xnT_copied, xnT_split = sem("xnT_mm"), sem("xnT_copied"), sem("xnT_split")
        xnT_rounded, prob_split, v_lo_ready = sem("xnT_rounded"), sem("prob_split"), sem("v_lo_ready")
        v_hi_ready, constant_parts = sem("v_hi_ready"), sem("constant_parts")
        w1_hi_ready, w1_lo_ready = sem("w1_hi_ready"), sem("w1_lo_ready")
        w2_hi_ready, w2_lo_ready = sem("w2_hi_ready"), sem("w2_lo_ready")
        w_spread = [sem(f"w_spread_{i}") for i in range(RING)]
        h_split, weighted, ffn_mm, ffn_added = sem("h_split"), sem("weighted"), sem("ffn_mm"), sem("ffn_added")
        gate_mm, gap_ready, gap_exp = sem("gate_mm"), sem("gap_ready"), sem("gap_exp")
        gate_ready, wT_mm, wT_copied = sem("gate_ready"), sem("wT_mm"), sem("wT_copied")
        b1_mm, b1T_ready = sem("b1_mm"), sem("b1T_ready")
        bn_done = sem("bn_done")
        rows_split = sem("rows_split")
        o_copied, sums_spread, inverted = sem("o_copied"), sem("sums_spread"), sem("inverted")
        inv_gathered, inv_spread = sem("inv_gathered"), sem("inv_spread")
        h_mm, gelu_done, y_mm, y_added = sem("h_mm"), sem("gelu_done"), sem("y_mm"), sem("y_added")
        lat_mm, lat_copied = sem("lat_mm"), sem("lat_copied")
        wpair_loaded = sem("wpair_loaded")
        wo_loaded, yT_cleared = sem("wo_loaded"), sem("yT_cleared")
        proj_mm, staged = sem("proj_mm"), sem("staged")
        hi_ready, lo_ready, dup_loaded = sem("hi_ready"), sem("lo_ready"), sem("dup_loaded")
        mx_mm, mx_read, max_ready = sem("mx_mm"), sem("mx_read"), sem("max_ready")
        rows_ready, rows_loaded = sem("rows_ready"), sem("rows_loaded")
        st_mm, exp_done, pv_mm, normalised = sem("st_mm"), sem("exp_done"), sem("pv_mm"), sem("normalised")
        op_mm, op_added, returned_mm, returned = (
            sem("op_mm"), sem("op_added"), sem("returned_mm"), sem("returned"))

        CR_GELU, CR_Y, CR_YA, CR_HS = HT, 2, 8, 2 * HT
        CR_ST, CR_PV, CR_O, CR_MX, CR_OP, CR_PS = 2, 4, 2, 2, 1, 2
        UNITS = 2 * GROUPS

        resid_flat = resid[:].rearrange("p a c -> p (a c)")
        x_tok = x.rearrange("o (a p) c -> p (o a) c", p=P)
        out_tok = out.rearrange("o (a p) c -> p (o a) c", p=P)
        block = ctx.enter_context(nc.Block())

        @block.sync
        def _(sp):
            for g in range(GROUPS):
                tiles = slice(g * GQ, g * GQ + GQ)
                sp.dma_start(resid[:, tiles, :], x_tok[:, tiles, :]).then_inc(x_loaded[g], 16)
            sp.dma_start(rw_sb[:], rW).then_inc(small_loaded, 16)
            sp.dma_start(rb_all[:], rb.rearrange("(a e) -> a e", a=1).broadcast_to([P, E])).then_inc(small_loaded, 16)
            sp.dma_start(b1_rows[0:S * HT, :], sb1.rearrange("e (h p) -> (e h) p", p=P)).then_inc(small_loaded, 16)
            sp.dma_start(b1_rows[S * HT:ALL * HT, :], b1.rearrange("e (h p) -> (e h) p", p=P)).then_inc(small_loaded, 16)
            sp.dma_start(b2_rows[0:S, :], sb2).then_inc(small_loaded, 16)
            sp.dma_start(b2_rows[S:ALL, :], b2).then_inc(small_loaded, 16)
            sp.dma_start(wdown[:], w_kv_down).then_inc(small_loaded, 16)

            def load_w1(f, e):
                if e >= 2 or f == 1:
                    sp.wait_ge(w1_lo_ready, f * ALL + e - 2 + 1)
                sp.dma_start(w1_raw(e), sW1[e] if e < S else W1[e - S]).then_inc(w1_loaded[e], 16)

            def load_w2(f, e):
                n = e if f == 0 else ALL + e - W2_KEPT
                if n >= 2:
                    sp.wait_ge(w2_lo_ready, n - 2 + 1)
                src = sW2[e] if e < S else W2[e - S]
                sp.dma_start(w2_raw(e), src.rearrange("(h p) d -> p h d", p=P)).then_inc(w2_loaded[e], 16)

            def spread_weight(f, g, e):
                y_at = (f * GROUPS + g) * ALL + e
                before = RING if e - S >= RING else RING + S
                sp.wait_ge(y_added, y_at - before + 1 + CR_YA)
                sp.dma_start(w_all[:, (e - S) % RING, :],
                             wT[e - S:e - S + 1, bass.ds(g * BANK, BANK)].rearrange("p (o c) -> p o c", o=1)
                             .broadcast_to([1, P, BANK])).then_inc(w_spread[(e - S) % RING], 16)

            def spread_weights(f):
                with sp.Fori(1, GROUPS) as g:
                    for e in range(S, ALL):
                        spread_weight(f, g, e)

            for e in range(ALL):
                load_w1(0, e)
                load_w2(0, e)
                if e == 5:
                    sp.wait_ge(wT_copied, GROUPS)
                if e >= 5:
                    spread_weight(0, 0, e - 3)
            for e in range(ALL - 3, ALL):
                spread_weight(0, 0, e)
            spread_weights(0)

            def load_wpair(pair):
                at = pair * P
                sp.dma_start(wpair[:, 1, :], w_q[:, bass.ds(at, P)]).then_inc(wpair_loaded, 16)
                sp.dma_start(wpair[:, 0, :], w_kv_up[:, bass.ds(at, P)]).then_inc(wpair_loaded, 16)
                sp.dma_start(wpair[:, 2, :], w_kv_up[:, bass.ds(at + HD, P)]).then_inc(wpair_loaded, 16)

            def duplicate(h, n):
                lo, hi = HALF[h]
                o_lo, o_hi = OTHER[h]
                sp.wait_ge(hi_ready, PIECES * n + PIECES)
                sp.dma_start(k_hi2[h][o_lo:o_hi, :].bitcast(F32), k_hi2[h][lo:hi, :].bitcast(F32)).then_inc(dup_loaded, 16)
                sp.dma_start(q_hi_m[h][0:DH, :].bitcast(F32), q_both[h][lo:hi, :].bitcast(F32)).then_inc(dup_loaded, 16)

            def max_rows(h, n):
                sp.wait_ge(rows_ready, n + 1)
                sp.dma_start(q_hi_m[h][DH:DH + 1, :].bitcast(F32), max_hi[:].bitcast(F32)).then_inc(rows_loaded, 16)
                sp.dma_start(q_hi_m[h][DH + 1:DH + 2, :].bitcast(F32), max_lo[:].bitcast(F32)).then_inc(rows_loaded, 16)

            load_wpair(0)
            duplicate("A", 0)
            max_rows("A", 0)

            def spread_inverse(p, u):
                unit = UNITS * p + u
                sp.wait_ge(o_copied, unit + 1 + CR_O)
                sp.dma_start(sums[:, u % 2, :], raw[DH:DH + 1, u % 2, :]).then_inc(sums_spread, 16)
                sp.wait_ge(inverted, unit + 1)
                sp.dma_start(inv_row[:, u % 2, :], inv_sums[:, u % 2, :]).then_inc(inv_gathered, 16)
                sp.wait_ge(inv_gathered, 16 * unit + 16)
                sp.dma_start(inv_all[u % 2][:], inv_row[:, u % 2:u % 2 + 1, :].broadcast_to([1, DH, BANK]))\
                  .then_inc(inv_spread, 16)

            def pair_body(p, first=False, last=False):
                if not last:
                    sp.wait_ge(proj_mm, PROJ * p + PROJ)
                    load_wpair(p + 1)
                if not first:
                    spread_inverse(p, -1)
                spread_inverse(p, 0)
                if not first:
                    sp.wait_ge(op_mm, GROUPS * p)
                sp.dma_start(wo_pair[:], w_out[bass.ds(p * P, P), :]).then_inc(wo_loaded, 16)
                duplicate("B", 2 * p + 1)
                spread_inverse(p, 1)
                spread_inverse(p, 2)
                max_rows("B", 2 * p + 1)
                spread_inverse(p, 3)
                spread_inverse(p, 4)
                if not last:
                    duplicate("A", 2 * p + 2)
                spread_inverse(p, 5)
                if last:
                    sp.wait_ge(lo_ready, PIECES * 2 * PAIRS)
                    sp.wait_ge(hi_ready, PIECES * 2 * PAIRS)
                    for e in range(T // HID):
                        load_w1(1, e)
                spread_inverse(p, 6)
                if not last:
                    max_rows("A", 2 * p + 2)

            pair_body(0, first=True)
            with sp.Fori(1, PAIRS - 1) as p:
                pair_body(p)
            pair_body(PAIRS - 1, last=True)
            spread_inverse(PAIRS, -1)
            for e in range(T // HID, ALL):
                load_w1(1, e)
            for e in range(W2_KEPT, W2_KEPT + 2):
                load_w2(1, e)
            sp.wait_ge(wT_copied, 2 * GROUPS)
            for e in range(S, ALL):
                spread_weight(1, 0, e)
                if S + 2 <= e < S + 4:
                    load_w2(1, e - S - 2 + W2_KEPT + 2)
            spread_weights(1)
            for g in range(GROUPS):
                sp.wait_ge(ffn_added, GROUPS + g + 1)
                tiles = slice(g * GQ, g * GQ + GQ)
                sp.dma_start(out_tok[:, tiles, :], resid[:, tiles, :]).then_inc(out_stored, 16)
            sp.wait_ge(out_stored, 16 * GROUPS)

        @block.gpsimd
        def _(pool):
            pool.memset(ident[:], 0.0).then_inc(pool_step, 1)
            pool.memset(mask_qk[:], 0.0).then_inc(pool_step, 1)
            pool.memset(mask_kq[:], 0.0).then_inc(pool_step, 1)
            pool.memset(minus_half[:], -0.5).then_inc(pool_step, 1)
            pool.wait_ge(pool_step, 4)
            pool.affine_select(out=ident[:], in_=ident[:], compare_op=ALU.not_equal, fill=1.0, base=0,
                               pattern=[[-1, P]], channel_multiplier=1).then_inc(pool_step, 1)
            pool.affine_select(out=mask_qk[:], in_=mask_qk[:], compare_op=ALU.is_ge, fill=NEG, base=0,
                               pattern=[[-1, P]], channel_multiplier=1).then_inc(pool_step, 1)
            pool.affine_select(out=mask_kq[:], in_=mask_kq[:], compare_op=ALU.is_ge, fill=NEG, base=0,
                               pattern=[[1, P]], channel_multiplier=-1).then_inc(pool_step, 1)
            pool.memset(euler[:], float(np.e)).then_inc(pool_step, 1)
            pool.wait_ge(pool_step, 8)

            def surroundings(h, done, signal):
                for n, (tile, value) in enumerate(((k_lo_1[h][DH:DH + 2, :], -1.0),
                                                   (v_hi_one[h][:, :, DH:DH + 1], 1.0),
                                                   (v_lo_0[h][:, :, DH:DH + 1], 0.0))):
                    pool.memset(tile.bitcast(F32), value).then_inc(signal, 1)
                    pool.wait_ge(signal, done + n + 1)

            for e in range(E):
                pool.memset(rev[:, e:e + 1], float(E - e)).then_inc(pool_step, 1)
            pool.wait_ge(pool_step, 8 + E)
            pool.tensor_copy(ident_b[:], ident[:]).then_inc(consts_ready, 1)

            def rstd(norm):
                for g in range(GROUPS):
                    tiles = slice(g * GQ, g * GQ + GQ)
                    pool.wait_ge(var_ready, GROUPS * norm + g + 1)
                    pool.tensor_tensor(stat[:, 4, tiles], stat[:, 3, tiles], minus_half[:, tiles], ALU.pow)\
                        .then_inc(rstd_ready, 1)

            def second_choice(f):
                pool.wait_ge(gap_ready, f + 1)
                pool.tensor_tensor(stat[:, 4, :], euler[:], stat[:, 0, :], ALU.pow).then_inc(gap_exp, 1)

            def lo_w1(f, e):
                pool.wait_ge(w1_hi_ready, f * ALL + e + 1)
                pool.tensor_tensor(w1_lo[:, e, :], w1_raw(e), w1_hi[:, e, :].bitcast(F32),
                                   ALU.subtract).then_inc(w1_lo_ready, 1)

            def lo_w2(f, e):
                pool.wait_ge(w2_loaded[e], 16 * f + 16)
                pool.wait_ge(w2_hi_ready, e + 1)
                pool.tensor_tensor(w2_lo(e), w2_raw(e), w2_hi[:, e, :, :].bitcast(F32),
                                   ALU.subtract).then_inc(w2_lo_ready, 1)

            def split_w1(e):
                pool.wait_ge(w1_loaded[e], 32)
                pool.tensor_copy(w1_hi[:, e, :], w1_raw(e)).then_inc(w1_hi_ready, 1)
                lo_w1(1, e)

            rstd(0)
            lo_w1(0, 0)
            lo_w1(0, 1)
            for e in range(ALL):
                lo_w2(0, e)
                if e == 0:
                    second_choice(0)
                if e + 2 < ALL:
                    lo_w1(0, e + 2)
            rstd(1)
            pool.wait_ge(ffn_mm, GROUPS)
            pool.memset(yT[:], 0.0).then_inc(yT_cleared, 1)
            pool.wait_ge(yT_cleared, 1)
            pool.wait_ge(lat_mm, GROUPS)
            surroundings("A", 0, constant_parts)
            surroundings("B", 3, constant_parts)

            def split_lo(h, n, m, pair):
                lo, hi = HALF[h]
                o_lo, o_hi = (0, DH) if m % 2 == 0 else OTHER[h]
                dst, rounded = ((k_lo_1, k_hi2), (q_both, q_both))[m % 2]
                cols = slice(m // 2 * BANK, (m // 2 + 1) * BANK)
                pool.wait_ge(staged, PROJ * pair + m + 1)
                pool.wait_ge(hi_ready, PIECES * n + m + 1)
                pool.tensor_tensor(dst[h][o_lo:o_hi, cols], qk_stage[lo:hi, m % 2, cols],
                                   rounded[h][lo:hi, cols].bitcast(F32), ALU.subtract).then_inc(lo_ready, 1)
                pool.wait_ge(lo_ready, PIECES * n + m + 1)

            def split_v_B(p, half):
                tiles = slice(half * TILES // 2, (half + 1) * TILES // 2)
                pool.wait_ge(v_hi_ready, V_STEPS * p + GROUPS + half + 1)
                pool.tensor_tensor(v_lo_0["B"][:, tiles, 0:DH], v_stage[:, tiles, :],
                                   v_hi_one["B"][:, tiles, 0:DH].bitcast(F32), ALU.subtract).then_inc(v_lo_ready, 1)
                pool.wait_ge(v_lo_ready, V_STEPS * p + GROUPS + half + 1)

            def pair_body(p, last=False):
                for m in range(PIECES):
                    split_lo("B", 2 * p + 1, m, p)
                for half in range(len(V_SLOTS)):
                    split_v_B(p, half)
                if not last:
                    for m in range(PIECES):
                        split_lo("A", 2 * p + 2, m, p + 1)

            for m in range(PIECES):
                split_lo("A", 0, m, 0)
            with pool.Fori(0, PAIRS - 1) as p:
                pair_body(p)
            pair_body(PAIRS - 1, last=True)
            pool.wait_ge(pv_mm, 2 * NS * (PAIRS - 1) + NS + CR_PV)
            for e in range(T // HID):
                split_w1(e)
            rstd(2)
            pool.wait_ge(pv_mm, 2 * NS * PAIRS + CR_PV)
            for e in range(T // HID, ALL):
                split_w1(e)
                if e == T // HID:
                    second_choice(1)
            for e in range(W2_KEPT, ALL):
                lo_w2(1, e)

        @block.scalar
        def _(act):
            act.sem_inc(gelu_done, CR_GELU)
            act.sem_inc(exp_done, CR_ST)
            act.sem_inc(o_copied, CR_O)

            def copy_xnT(norm, rounded=False, groups=range(GROUPS)):
                for g in groups:
                    cols = slice(g * BANK, (g + 1) * BANK)
                    act.wait_ge(xnT_mm, GROUPS * norm + g + 1)
                    act.activation(xnT[:, cols], bank[g][:], ACT.Copy).then_inc(xnT_copied, 1)
                    if rounded:
                        act.activation(xnT_hi[:, cols], bank[g][:], ACT.Copy).then_inc(xnT_rounded, 1)

            def ffn(f):
                copy_xnT(2 * f, rounded=True)
                act.wait_ge(b1T_ready, 1)

                def group(g, first=False):
                    for e in range(ALL):
                        y_at = (f * GROUPS + g) * ALL + e
                        act.wait_ge(y_mm, y_at - 2 + 1 + CR_Y)
                        for ht in range(HT):
                            at = y_at * HT + ht
                            act.wait_ge(h_mm, at + 1)
                            act.wait_ge(h_split, at - 2 * HT + 1 + CR_HS)
                            act.activation(hbuf[:, e % 2 * HT + ht, :], bank[ht][:], ACT.Gelu,
                                           bias=b1T[:, e, ht:ht + 1])
                            act.activation(h_hi[e % 2][:, ht, :], bank[ht][:], ACT.Gelu,
                                           bias=b1T[:, e, ht:ht + 1]).then_inc(gelu_done, 1)
                        if first and f == 0 and e + W1_AHEAD < ALL:
                            round_w1(e + W1_AHEAD)
                        if first and e in WT_AT:
                            for i in range(2):
                                n = 2 * WT_AT.index(e) + i
                                act.wait_ge(wT_mm, GROUPS * f + n + 1)
                                act.activation(wT[:, n * BANK:(n + 1) * BANK], bank[4 + i][0:E, :], ACT.Copy)\
                                   .then_inc(wT_copied, 1)

                group(0, first=True)
                with act.Fori(1, GROUPS) as g:
                    group(g)

            def round_w1(e):
                act.wait_ge(w1_loaded[e], 16)
                act.activation(w1_hi[:, e, :], w1_raw(e), ACT.Copy).then_inc(w1_hi_ready, 1)

            for e in range(W1_AHEAD):
                round_w1(e)
            ffn(0)

            def round_piece(h, m, src):
                lo, hi = HALF[h]
                dst = (k_hi2, q_both)[m % 2][h]
                act.activation(dst[lo:hi, m // 2 * BANK:(m // 2 + 1) * BANK], src, ACT.Copy).then_inc(hi_ready, 1)

            def stage(pair, k):
                act.wait_ge(proj_mm, PROJ * pair + k + 1)
                if k < PIECES:
                    lo, hi = HALF["A"]
                    round_piece("A", k, proj_bank(k)[lo:hi, :])
                    act.activation(qk_stage[:, k % 2, k // 2 * BANK:(k // 2 + 1) * BANK], proj_bank(k)[:], ACT.Copy)\
                       .then_inc(staged, 1)
                else:
                    tiles = slice(GQ * (k - PIECES), GQ * (k - PIECES) + GQ)
                    v = proj_bank(k)[:].rearrange("p (a d) -> p a d", a=GQ)
                    act.activation(v_hi_one["A"][:, tiles, 0:DH], v[:, :, 0:DH], ACT.Copy).then_inc(v_hi_ready, 1)
                    act.activation(v_stage[:, tiles, :], v[:, :, DH:P], ACT.Copy).then_inc(staged, 1)

            act.wait_ge(y_added, GROUPS * ALL + CR_YA)
            copy_xnT(1, groups=[0])
            for g in range(GROUPS):
                if g + 1 < GROUPS:
                    copy_xnT(1, groups=[g + 1])
                act.wait_ge(lat_mm, g + 1)
                act.activation(latT[:, g * BANK:(g + 1) * BANK], bank[g][:], ACT.Copy).then_inc(lat_copied, 1)
                stage(0, 2 * g)
                stage(0, 2 * g + 1)
            for k in range(PIECES, PROJ):
                stage(0, k)

            def round_v(p, half):
                tiles = slice(half * TILES // 2, (half + 1) * TILES // 2)
                act.activation(v_hi_one["B"][:, tiles, 0:DH], v_stage[:, tiles, :], ACT.Copy).then_inc(v_hi_ready, 1)

            def copy_output(p, u):
                unit = UNITS * p + u
                last_step = NS * (u // GROUPS) + UNIT_LAST[u % GROUPS]
                act.wait_ge(pv_mm, 2 * NS * p + last_step + 1 + CR_PV)
                act.wait_ge(normalised, unit - 1 + CR_O)
                act.activation(raw[0:DH + 1, u % 2, :], bank[2 + u % 2][0:DH + 1, :], ACT.Copy).then_inc(o_copied, 1)

            def pair_body(p, first=False, last=False):
                for n in range(2 * NS):
                    s, head = n % NS, n // NS
                    g, j = STEPS[s]
                    at = max(GQ * g, j)
                    width = (GQ * g + GQ - at) * P
                    act.wait_ge(st_mm, 2 * NS * p + n + 1)
                    act.wait_ge(prob_split, 2 * NS * p + n - 2 + 1 + CR_PS)
                    act.activation(prob[:, n % 2, 0:width], bank[n % 2][:, 0:width], ACT.Exp, scale=SCALE)
                    act.wait_ge(pv_mm, 2 * NS * p + n - 4 + 1 + CR_PV)
                    act.activation(prob_hi[:, n % 4, 0:width], bank[n % 2][:, 0:width], ACT.Exp, scale=SCALE)\
                       .then_inc(exp_done, 1)
                    u = unit_ended(n - COPY_LAG)
                    if u is not None and not (first and u < 0):
                        copy_output(p, u)
                    if head == 0 and s < PIECES:
                        lo, hi = HALF["B"]
                        round_piece("B", s, qk_stage[lo:hi, s % 2, s // 2 * BANK:(s // 2 + 1) * BANK])
                    if head == 0 and s in V_SLOTS:
                        if s == V_SLOTS[0]:
                            act.wait_ge(pv_mm, 2 * NS * p + CR_PV)
                        round_v(p, V_SLOTS.index(s))
                    if head == 1 and s < PROJ and not last:
                        if s == 0:
                            act.wait_ge(lo_ready, PIECES * (2 * p + 2))
                        if s == PIECES:
                            act.wait_ge(v_lo_ready, V_STEPS * p + V_STEPS)
                        stage(p + 1, s)

            pair_body(0, first=True)
            with act.Fori(1, PAIRS - 1) as p:
                pair_body(p)
            pair_body(PAIRS - 1, last=True)
            copy_output(PAIRS, -1)
            ffn(1)

        @block.vector
        def _(dve):
            step = [0]

            def link(ins):
                step[0] += 1
                ins.then_inc(dve_step, 1)
                dve.wait_ge(dve_step, step[0])

            def over_experts(ap):
                return ap.rearrange("p (a o) -> p a o", o=1).broadcast_to([P, TILES, E])

            def stats(n, g):
                tiles = slice(g * GQ, g * GQ + GQ)
                for t in range(g * GQ, g * GQ + GQ):
                    dve.bn_stats(bn[:, t, :], resid[:, t, :]).then_inc(bn_done, 1)
                for t in range(g * GQ, g * GQ + GQ):
                    dve.wait_ge(bn_done, TILES * n + t + 1)
                    ins = dve.bn_aggr(mean_var[:, t, :], bn[:, t, :])
                link(ins)
                dve.tensor_scalar(stat[:, 3, tiles], mean_var[:, tiles, 1], EPS, None, ALU.add).then_inc(var_ready, 1)

            def apply(n, g):
                dve.wait_ge(rstd_ready, GROUPS * n + g + 1)
                for t in range(g * GQ, g * GQ + GQ):
                    ins = dve.tensor_scalar(xn[:, t, :], resid[:, t, :], mean_var[:, t, 0:1], stat[:, 4, t:t + 1],
                                            ALU.subtract, ALU.mult)
                ins.then_inc(xn_ready, 1)

            def add_back(f, g):
                dve.wait_ge(ffn_mm, GROUPS * f + g + 1)
                part = resid_flat[:, g * BANK:(g + 1) * BANK]
                dve.tensor_tensor(part, bank[g][:], part, ALU.add).then_inc(ffn_added, 1)
                dve.wait_ge(ffn_added, GROUPS * f + g + 1)

            def ffn(f):
                for g in range(GROUPS):
                    cols = slice(g * BANK, (g + 1) * BANK)
                    dve.wait_ge(xnT_copied, GROUPS * 2 * f + g + 1)
                    dve.wait_ge(xnT_rounded, GROUPS * f + g + 1)
                    ins = dve.tensor_tensor(xnT_lo[:, cols], xnT[:, cols], xnT_hi[:, cols].bitcast(F32), ALU.subtract)
                ins.then_inc(xnT_split, 1)
                if f == 0:
                    round_w2(0)
                    dve.wait_ge(b1_mm, 1)
                    link(dve.tensor_copy(b2T[:], bank[5][:, ALL * HT:ALL * HT + ALL]))
                    dve.tensor_copy(b1T[:].rearrange("p e h -> p (e h)"), bank[5][:, 0:ALL * HT]).then_inc(b1T_ready, 1)
                choices(f)
                group(0, f, first=True)
                with dve.Fori(1, GROUPS) as g:
                    group(g, f)
                weigh_output(GROUPS - 1, ALL - 1, f)

            G, EQ, KEY, OH1, G2, OH2, W = range(7)

            def choices(f):
                dve.wait_ge(gate_mm, f + 1)
                gates = bank[4][:, 0:TILES * E].rearrange("p (a e) -> p a e", e=E)
                rb_b = rb_all[:].rearrange("p (o e) -> p o e", o=1).broadcast_to([P, TILES, E])
                rev_b = rev[:].rearrange("p (o e) -> p o e", o=1).broadcast_to([P, TILES, E])
                link(dve.tensor_tensor(gate[:, G], gates, rb_b, ALU.add))
                for src, best, onehot in ((G, 1, OH1), (G2, 2, OH2)):
                    if src == G2:
                        link(dve.scalar_tensor_tensor(out=gate[:, G2], in0=gate[:, OH1], scalar=-BIG,
                                                      in1=gate[:, G], op0=ALU.mult, op1=ALU.add))
                    link(dve.reduce_max(stat[:, best, :], gate[:, src], axis=AX.X))
                    link(dve.tensor_tensor(gate[:, EQ], gate[:, src], over_experts(stat[:, best, :]), ALU.is_equal))
                    link(dve.tensor_tensor(gate[:, KEY], gate[:, EQ], rev_b, ALU.mult))
                    link(dve.reduce_max(stat[:, 5, :], gate[:, KEY], axis=AX.X))
                    link(dve.tensor_tensor(gate[:, onehot], gate[:, KEY], over_experts(stat[:, 5, :]), ALU.is_equal))
                dve.tensor_tensor(stat[:, 0, :], stat[:, 2, :], stat[:, 1, :], ALU.subtract).then_inc(gap_ready, 1)

            def weights(f):
                dve.wait_ge(gap_exp, f + 1)
                ex = stat[:, 4, :]
                link(dve.tensor_scalar(stat[:, 3, :], ex, 1.0, None, ALU.add))
                link(dve.reciprocal(stat[:, 5, :], stat[:, 3, :]))
                link(dve.tensor_scalar(stat[:, 1, :], stat[:, 5, :], 0.5, None, ALU.mult))
                link(dve.tensor_tensor(stat[:, 2, :], ex, stat[:, 1, :], ALU.mult))
                link(dve.tensor_tensor(gate[:, EQ], gate[:, OH1], over_experts(stat[:, 1, :]), ALU.mult))
                link(dve.tensor_tensor(gate[:, KEY], gate[:, OH2], over_experts(stat[:, 2, :]), ALU.mult))
                dve.tensor_tensor(gate[:, W], gate[:, EQ], gate[:, KEY], ALU.add).then_inc(gate_ready, 1)

            def weigh_output(g, e, f):
                y_at = (f * GROUPS + g) * ALL + e
                sums = yT[:, bass.ds(g * BANK, BANK)]
                dve.wait_ge(y_mm, y_at + 1 + CR_Y)
                y, bias = bank[6 + e % 2][:], b2T[:, e:e + 1]
                if e == 0:
                    dve.tensor_scalar(sums, y, bias, 0.5 / S, ALU.add, ALU.mult).then_inc(y_added, 1)
                    return
                if e < S:
                    ins = dve.tensor_scalar(product[:, e % 2, :], y, bias, 0.5 / S, ALU.add, ALU.mult)
                else:
                    slot = (e - S) % RING
                    uses = (f * GROUPS + g) * (E // RING) + (e - S) // RING
                    dve.wait_ge(w_spread[slot], 16 * uses + 16)
                    ins = dve.scalar_tensor_tensor(out=product[:, e % 2, :], in0=y, scalar=bias,
                                                   in1=w_all[:, slot, :], op0=ALU.add, op1=ALU.mult)
                ins.then_inc(weighted, 1)
                dve.wait_ge(weighted, (f * GROUPS + g) * (ALL - 1) + e)
                dve.wait_ge(y_added, y_at + CR_YA)
                dve.tensor_tensor(sums, sums, product[:, e % 2, :], ALU.add).then_inc(y_added, 1)

            def group(g, f, first=False):
                for e in range(ALL):
                    y_at = (f * GROUPS + g) * ALL + e
                    dve.wait_ge(y_mm, y_at - 2 + 1 + CR_Y)
                    for ht in range(HT):
                        dve.wait_ge(gelu_done, y_at * HT + ht + 1 + CR_GELU)
                        dve.tensor_tensor(h_lo[e % 2][:, ht, :], hbuf[:, e % 2 * HT + ht, :],
                                          h_hi[e % 2][:, ht, :].bitcast(F32), ALU.subtract).then_inc(h_split, 1)
                    if first and f == 0 and e + 1 < ALL:
                        round_w2(e + 1)
                    if first and e == 0:
                        weights(f)
                    if e >= 1:
                        weigh_output(g, e - 1, f)
                    elif not first:
                        weigh_output(g - 1, ALL - 1, f)

            def round_w2(e):
                dve.wait_ge(w2_loaded[e], 16)
                dve.tensor_copy(w2_hi[:, e, :, :], w2_raw(e)).then_inc(w2_hi_ready, 1)

            dve.sem_inc(prob_split, CR_PS)
            dve.sem_inc(y_added, CR_YA)
            dve.sem_inc(h_split, CR_HS)
            dve.sem_inc(mx_read, CR_MX)
            dve.sem_inc(op_added, CR_OP)
            dve.sem_inc(normalised, CR_O)
            for g in range(GROUPS):
                dve.wait_ge(x_loaded[g], 16)
                stats(0, g)
                if g:
                    apply(0, g - 1)
            apply(0, GROUPS - 1)
            ffn(0)
            for g in range(GROUPS):
                add_back(0, g)
                stats(1, g)
                if g:
                    apply(1, g - 1)
            apply(1, GROUPS - 1)
            dve.wait_ge(yT_cleared, 1)
            link(dve.memset(max_part[:], -BIG))

            def reduce_chunk(h, n, c):
                i, part = CHUNKS[c]
                width = min(BANK, (i + 1) * P - part * BANK)
                dve.wait_ge(mx_mm, MU * n + c + 1)
                ring = max_ring(h, n)
                dve.reduce_max(max_part[:, i, part:part + 1], bank[ring[c % len(ring)]][:, 0:width], axis=AX.X)\
                   .then_inc(mx_read, 1)

            def reduce_last(n):
                dve.wait_ge(mx_read, MU * n + NC + CR_MX)
                dve.reduce_max(max_q[:], max_part[:], axis=AX.X).then_inc(max_ready, 1)

            def split_rows(h, n, first=False):
                src = bank[4][0:TILES, 0:P]
                dve.wait_ge(mx_mm, MU * n + NC + 1)
                if not first:
                    dve.wait_ge(rows_loaded, 32 * n)
                dve.tensor_copy(max_hi[:], src).then_inc(rows_split, 1)
                dve.wait_ge(rows_split, n + 1)
                dve.tensor_tensor(max_lo[:], src, max_hi[:].bitcast(F32), ALU.subtract).then_inc(mx_read, 1)
                dve.wait_ge(mx_read, MU * n + MU + CR_MX)
                dve.sem_inc(rows_ready, 1)

            def invert(p, u):
                unit = UNITS * p + u
                dve.wait_ge(sums_spread, 16 * unit + 16)
                if not (isinstance(p, int) and unit < 2):
                    dve.wait_ge(inv_gathered, 16 * (unit - 1))
                dve.reciprocal(inv_sums[:, u % 2, :], sums[:, u % 2, :]).then_inc(inverted, 1)

            def normalise(p, u):
                unit, g = UNITS * p + u, u % GROUPS
                lo, hi = HALF["AB"[u // GROUPS % 2]]
                dve.wait_ge(inv_spread, 16 * unit + 16)
                if not (isinstance(p, int) and p == 0) and 0 <= u < GROUPS:
                    dve.wait_ge(op_mm, GROUPS * (p - 1) + g + 1)
                dve.tensor_tensor(oT[lo:hi, g, :], raw[0:DH, u % 2, :], inv_all[u % 2][:], ALU.mult)\
                   .then_inc(normalised, 1)

            def add_projected(p, g):
                dve.wait_ge(op_mm, GROUPS * p + g + 1)
                dve.wait_ge(op_added, GROUPS * p + g + CR_OP)
                part = yT[:, g * BANK:(g + 1) * BANK]
                dve.tensor_tensor(part, bank[7][:], part, ALU.add).then_inc(op_added, 1)

            def return_group(g):
                dve.wait_ge(returned_mm, g + 1)
                part = resid_flat[:, g * BANK:(g + 1) * BANK]
                dve.tensor_tensor(part, bank[4 + g % 2][:], part, ALU.add).then_inc(returned, 1)

            def split_v_A(pair, i):
                tiles = slice(GQ * i, GQ * i + GQ)
                v = proj_bank(PIECES + i)[:].rearrange("p (a d) -> p a d", a=GQ)[:, :, 0:DH]
                dve.wait_ge(v_hi_ready, V_STEPS * pair + i + 1)
                dve.wait_ge(staged, PROJ * pair + PIECES + i + 1)
                dve.tensor_tensor(v_lo_0["A"][:, tiles, 0:DH], v, v_hi_one["A"][:, tiles, 0:DH].bitcast(F32),
                                  ALU.subtract).then_inc(v_lo_ready, 1)

            def split_prob(p, n):
                g, j = STEPS[n % NS]
                width = (GQ * g + GQ - max(GQ * g, j)) * P
                dve.wait_ge(exp_done, 2 * NS * p + n + 1 + CR_ST)
                dve.wait_ge(pv_mm, 2 * NS * p + n - 2 + 1 + CR_PV)
                dve.tensor_tensor(prob_lo[:, n % 2, 0:width], prob[:, n % 2, 0:width],
                                  prob_hi[:, n % 4, 0:width].bitcast(F32), ALU.subtract).then_inc(prob_split, 1)

            for g in range(GROUPS):
                for c in chunks_of(g):
                    reduce_chunk("A", 0, c)
                if g >= GROUPS - 2:
                    for i in range(2):
                        split_v_A(0, 2 * (g - GROUPS + 2) + i)
            reduce_last(0)
            split_rows("A", 0, first=True)

            def pair_body(p, first=False, last=False):
                for n in range(2 * NS):
                    s, head = n % NS, n // NS
                    here, nxt = "AB"[head], "BA"[head]
                    number = 2 * p + 1 + head
                    if not (first and n == 0):
                        split_prob(p, n - 1)
                    if not (last and head == 1):
                        if head == 1 and PIECES + SPLIT_LAG <= s < PROJ + SPLIT_LAG:
                            split_v_A(p + 1, s - SPLIT_LAG - PIECES)
                        for c in range(NC):
                            if CHUNK_SLOTS[here][c] == s:
                                reduce_chunk(nxt, number, c)
                        if s == MAX_SLOT:
                            reduce_last(number)
                        if s == ROW_SLOT:
                            split_rows(nxt, number)
                    u = unit_ended(n - INVERT_LAG)
                    if u is not None and not (first and u < 0):
                        invert(p, u)
                    u = unit_ended(n - NORM_LAG)
                    if u is not None and not (first and u < 0):
                        normalise(p, u)
                    u = unit_ended(n - PROJECT_LAG - 1)
                    if u is not None and u < 0 and not first:
                        add_projected(p - 1, GROUPS - 1)
                    if u is not None and u >= GROUPS:
                        add_projected(p, u - GROUPS)
                    u = unit_ended(n - RETURN_LAG)
                    if last and u is not None and u >= GROUPS:
                        return_group(u - GROUPS)

            pair_body(0, first=True)
            with dve.Fori(1, PAIRS - 1) as p:
                pair_body(p)
            pair_body(PAIRS - 1, last=True)
            split_prob(PAIRS, -1)
            stats(2, 0)
            stats(2, 1)
            apply(2, 0)
            invert(PAIRS, -1)
            stats(2, 2)
            apply(2, 1)
            apply(2, 2)
            normalise(PAIRS, -1)
            add_projected(PAIRS - 1, GROUPS - 1)
            return_group(GROUPS - 1)
            dve.wait_ge(returned, GROUPS)
            stats(2, 3)
            apply(2, 3)
            ffn(1)
            for g in range(GROUPS):
                add_back(1, g)

        @block.tensor
        def _(pe):
            pe.sem_inc(y_mm, CR_Y)
            pe.sem_inc(pv_mm, CR_PV)

            def three_pass(dst, l_hi, l_lo, r_hi, r_lo):
                pe.matmul(dst, l_hi, r_hi, start=True, stop=False)
                pe.matmul(dst, l_hi, r_lo, start=False, stop=False)
                return pe.matmul(dst, l_lo, r_hi, start=False, stop=True)

            def keep_warm(count):
                for _ in range(count):
                    pe.matmul(bank[7][:, 0:2 * P], ident_b[:], ident[:].bitcast(BF16), start=True, stop=True)

            def gates(f, g):
                pe.wait_ge(xnT_copied, GROUPS * 2 * f + g + 1)
                for t in range(g * GQ, g * GQ + GQ):
                    ins = pe.matmul(bank[4][:, t * E:(t + 1) * E], xnT[:, t * P:(t + 1) * P], rw_sb[:],
                                    start=True, stop=True)
                if g == GROUPS - 1:
                    ins.then_inc(gate_mm, 1)

            def transpose_xn(n, groups=range(GROUPS)):
                for g in groups:
                    pe.wait_ge(xn_ready, GROUPS * n + g + 1)
                    for t in range(GQ):
                        ins = pe.transpose(bank[g][:, t * P:(t + 1) * P], xn[:, g * GQ + t, :], ident[:])
                    ins.then_inc(xnT_mm, 1)

            def ffn(f):
                if f == 0:
                    pe.wait_ge(small_loaded, 16 * 7)
                    for g in range(GROUPS - 1):
                        transpose_xn(0, [g])
                        if g:
                            gates(0, g - 1)
                        keep_warm(4)
                transpose_xn(2 * f, [GROUPS - 1])
                if f == 0:
                    gates(0, GROUPS - 2)
                if f == 0:
                    pe.wait_ge(small_loaded, 16 * 7)
                    pe.transpose(bank[5][:, 0:ALL * HT], b1_rows, ident[0:ALL * HT, 0:ALL * HT])
                    pe.transpose(bank[5][:, ALL * HT:ALL * HT + ALL], b2_rows, ident[0:ALL, 0:ALL]).then_inc(b1_mm, 1)
                gates(f, GROUPS - 1)
                pe.wait_ge(xnT_split, f + 1)

                def second_layer(g, e):
                    y_at = (f * GROUPS + g) * ALL + e
                    if f == 0 or e >= W2_KEPT:
                        pe.wait_ge(w2_lo_ready, f * (ALL - W2_KEPT) + e + 1)
                    pe.wait_ge(h_split, y_at * HT + HT + CR_HS)
                    pe.wait_ge(y_added, y_at - 2 + 1 + CR_YA)
                    dst = bank[6 + e % 2][:]
                    for ht in range(HT):
                        hi, lo = h_hi[e % 2][:, ht, :], h_lo[e % 2][:, ht, :]
                        pe.matmul(dst, w2_hi[:, e, ht, :], hi, start=ht == 0, stop=False)
                        pe.matmul(dst, w2_hi[:, e, ht, :], lo, start=False, stop=False)
                        ins = pe.matmul(dst, w2_lo(e)[:, ht, :], hi, start=False, stop=ht == HT - 1)
                    ins.then_inc(y_mm, 1)

                def group(g, first=False):
                    x_hi = xnT_hi[:, bass.ds(g * BANK, BANK)]
                    x_lo = xnT_lo[:, bass.ds(g * BANK, BANK)]
                    for e in range(ALL):
                        pe.wait_ge(w1_lo_ready, f * ALL + e + 1)
                        for ht in range(HT):
                            at = ((f * GROUPS + g) * ALL + e) * HT + ht
                            pe.wait_ge(gelu_done, at - HT + 1 + CR_GELU)
                            cols = slice(ht * P, (ht + 1) * P)
                            three_pass(bank[ht][:], w1_hi[:, e, cols], w1_lo[:, e, cols], x_hi, x_lo)\
                                .then_inc(h_mm, 1)
                        if e >= 1:
                            second_layer(g, e - 1)
                        elif not first:
                            second_layer(g - 1, ALL - 1)
                        if first and e in WT_AT:
                            pe.wait_ge(gate_ready, f + 1)
                            for i in range(2):
                                n = 2 * WT_AT.index(e) + i
                                if n >= 2:
                                    pe.wait_ge(wT_copied, GROUPS * f + n - 1)
                                for t in range(GQ):
                                    ins = pe.transpose(bank[4 + i][0:E, t * P:(t + 1) * P],
                                                       gate[:, 6, n * GQ + t, :], ident[:])
                                ins.then_inc(wT_mm, 1)

                group(0, first=True)
                with pe.Fori(1, GROUPS) as g:
                    group(g)
                second_layer(GROUPS - 1, ALL - 1)
                pe.wait_ge(gelu_done, (f + 1) * GROUPS * ALL * HT + CR_GELU)
                for g in range(GROUPS):
                    pe.wait_ge(y_added, (f * GROUPS + g + 1) * ALL + CR_YA)
                    for t in range(GQ):
                        tile = g * GQ + t
                        ins = pe.transpose(bank[g][:, t * P:(t + 1) * P], yT[:, tile * P:(tile + 1) * P], ident[:])
                    ins.then_inc(ffn_mm, 1)

            pe.wait_ge(consts_ready, 1)
            keep_warm(22)
            ffn(0)

            def project(pair, k):
                if k == 0:
                    pe.wait_ge(wpair_loaded, 48 * pair + 48)
                if k >= 2:
                    pe.wait_ge(staged, PROJ * pair + k - 1)
                if k >= PIECES + 2:
                    pe.wait_ge(v_lo_ready, V_STEPS * pair + k - PIECES - 1)
                if k == 1 and not (isinstance(pair, int) and pair == 0):
                    pe.wait_ge(op_added, GROUPS * (pair - 1) + CR_OP)
                if k == 0 and not (isinstance(pair, int) and pair == 0):
                    pe.wait_ge(staged, PROJ * pair)
                    pe.wait_ge(mx_read, MU * 2 * pair + CR_MX)
                if k < PIECES:
                    src = latT if k % 2 == 0 else xnT
                    pe.matmul(proj_bank(k)[:], wpair[:, k % 2, :], src[:, k // 2 * BANK:(k // 2 + 1) * BANK],
                              start=True, stop=True).then_inc(proj_mm, 1)
                else:
                    for t in range(GQ):
                        tile = GQ * (k - PIECES) + t
                        ins = pe.matmul(proj_bank(k)[:, t * P:(t + 1) * P], latT[:, tile * P:(tile + 1) * P],
                                        wpair[:, 2, :], start=True, stop=True)
                    ins.then_inc(proj_mm, 1)

            def max_chunk(h, n, c, pair=0):
                i, part = CHUNKS[c]
                lo, hi = HALF[h]
                width = min(BANK, (i + 1) * P - part * BANK)
                diagonal = part == i // GQ
                ring = max_ring(h, n)
                dst = bank[ring[c % len(ring)]]
                if part == 0 and i % GQ == 0:
                    pe.wait_ge(hi_ready, PIECES * n + 2 * (i // GQ) + 2)
                if h == "B" and c == 2:
                    pe.wait_ge(staged, PROJ * (pair + 1))
                    pe.wait_ge(v_lo_ready, V_STEPS * pair + GROUPS)
                pe.wait_ge(mx_read, MU * n + max(c - len(ring) + 1, 0) + CR_MX)
                ins = pe.matmul(dst[:, 0:width], q_both[h][lo:hi, i * P:(i + 1) * P],
                                k_hi2[h][lo:hi, part * BANK:part * BANK + width], start=True, stop=not diagonal)
                if diagonal:
                    ins = pe.matmul(dst[:, width - P:width], ident_b[:], mask_qk[:], start=False, stop=True)
                ins.then_inc(mx_mm, 1)

            def max_transpose(h, n):
                pe.wait_ge(max_ready, n + 1)
                pe.wait_ge(mx_read, MU * n + NC + CR_MX)
                pe.transpose(bank[4][0:TILES, 0:P], max_q[:], ident[:]).then_inc(mx_mm, 1)

            transpose_xn(1, [0])
            for g in range(GROUPS):
                if g + 1 < GROUPS:
                    transpose_xn(1, [g + 1])
                pe.wait_ge(xnT_copied, GROUPS + g + 1)
                pe.matmul(bank[g][:], wdown[:], xnT[:, g * BANK:(g + 1) * BANK], start=True, stop=True)\
                  .then_inc(lat_mm, 1)
                if g >= 2:
                    for c in chunks_of(g - 2):
                        max_chunk("A", 0, c)
                pe.wait_ge(lat_copied, g + 1)
                project(0, 2 * g)
                project(0, 2 * g + 1)
            for g in range(GROUPS - 2, GROUPS):
                for c in chunks_of(g):
                    max_chunk("A", 0, c)
                for i in range(2):
                    project(0, PIECES + 2 * (g - GROUPS + 2) + i)
            max_transpose("A", 0)
            pe.wait_ge(constant_parts, 6)

            def scores(p, n):
                head, s = n // NS, n % NS
                h = "AB"[head]
                g, j = STEPS[s]
                at = max(GQ * g, j)
                width = (GQ * g + GQ - at) * P
                keys, queries = slice(j * P, (j + 1) * P), slice(at * P, at * P + width)
                diagonal = j >= GQ * g
                dst = bank[n % 2]
                if s == 0:
                    number = 2 * p + head
                    pe.wait_ge(lo_ready, PIECES * (number + 1))
                    pe.wait_ge(dup_loaded, 32 * number + 32)
                    pe.wait_ge(rows_loaded, 32 * number + 32)
                pe.wait_ge(exp_done, 2 * NS * p + n - 2 + 1 + CR_ST)
                pe.matmul(dst[:, 0:width], k_hi2[h][:, keys], q_both[h][:, queries], start=True, stop=False)
                ins = pe.matmul(dst[:, 0:width], k_lo_1[h][:, keys], q_hi_m[h][:, queries],
                                start=False, stop=not diagonal)
                if diagonal:
                    ins = pe.matmul(dst[:, 0:P], ident_b[:], mask_kq[:], start=False, stop=True)
                ins.then_inc(st_mm, 1)

            def weigh(p, n):
                head, s = n // NS, n % NS
                g, j = STEPS[s]
                at = max(GQ * g, j)
                u = GROUPS * head + g
                if j == 0:
                    pe.wait_ge(o_copied, UNITS * p + u - 2 + 1 + CR_O)
                if s == 0:
                    done = GROUPS if head % 2 == 0 else V_STEPS
                    pe.wait_ge(v_lo_ready, V_STEPS * p + done)
                pe.wait_ge(prob_split, 2 * NS * p + n + 1 + CR_PS)
                h = "AB"[head % 2]
                cols = slice(0, (GQ * g + GQ - at) * P)
                dst = bank[2 + u % 2][0:DH + 1, (at - GQ * g) * P:BANK]
                hi, lo = v_hi_one[h][:, j, :], v_lo_0[h][:, j, :]
                pe.matmul(dst, hi, prob_hi[:, n % 4, cols], start=j == 0, stop=False)
                pe.matmul(dst, lo, prob_hi[:, n % 4, cols], start=False, stop=False)
                pe.matmul(dst, hi, prob_lo[:, n % 2, cols], start=False,
                          stop=j == GQ * g + GQ - 1).then_inc(pv_mm, 1)

            def out_project(p, g, last=False):
                pe.wait_ge(normalised, UNITS * p + GROUPS + g + 1 + CR_O)
                pe.wait_ge(op_added, GROUPS * p + g + CR_OP)
                if g == 0:
                    pe.wait_ge(wo_loaded, 16 * p + 16)
                    pe.wait_ge(staged, PROJ * PAIRS if last else PROJ * (p + 2))
                    pe.wait_ge(v_lo_ready, V_STEPS * (PAIRS - 1) + GROUPS if last else V_STEPS * (p + 1) + GROUPS)
                pe.matmul(bank[7][:], wo_pair[:], oT[:, g, :], start=True, stop=True).then_inc(op_mm, 1)

            def return_group(g):
                pe.wait_ge(op_added, GROUPS * (PAIRS - 1) + g + 1 + CR_OP)
                if g == 0:
                    pe.wait_ge(mx_read, MU * 2 * PAIRS + CR_MX)
                if g >= 2:
                    pe.wait_ge(returned, g - 1)
                for t in range(GQ):
                    tile = g * GQ + t
                    ins = pe.transpose(bank[4 + g % 2][:, t * P:(t + 1) * P], yT[:, tile * P:(tile + 1) * P], ident[:])
                ins.then_inc(returned_mm, 1)

            def pair_body(p, first=False, last=False):
                for n in range(2 * NS):
                    s, head = n % NS, n // NS
                    here, nxt = "AB"[head], "BA"[head]
                    number = 2 * p + 1 + head
                    scores(p, n)
                    if not (last and head == 1):
                        if head == 1 and s < PROJ:
                            project(p + 1, s)
                        chunks = [c for c in range(NC) if CHUNK_SLOTS[here][c] == s]
                        for c in chunks[0:1]:
                            max_chunk(nxt, number, c, p)
                        if s == ROW_SLOT:
                            max_transpose(nxt, number)
                    if not (first and n < WEIGH_LAG):
                        weigh(p, n - WEIGH_LAG)
                    if not (last and head == 1):
                        for c in chunks[1:]:
                            max_chunk(nxt, number, c, p)
                    u = unit_ended(n - PROJECT_LAG)
                    if u is not None and u < 0 and not first:
                        out_project(p - 1, GROUPS - 1)
                    if u is not None and u >= GROUPS:
                        out_project(p, u - GROUPS, last)
                    u = unit_ended(n - RETURN_LAG)
                    if last and u is not None and u >= GROUPS:
                        return_group(u - GROUPS)

            pair_body(0, first=True)
            with pe.Fori(1, PAIRS - 1) as p:
                pair_body(p)
            pair_body(PAIRS - 1, last=True)
            for n in range(-WEIGH_LAG, 0):
                weigh(PAIRS, n)
            transpose_xn(2, range(GROUPS - 1))
            pe.wait_ge(returned, GROUPS - 1)
            for g in range(GROUPS - 1):
                gates(1, g)
            out_project(PAIRS - 1, GROUPS - 1)
            return_group(GROUPS - 1)
            ffn(1)


_INS = ["L0_attn_x", "L0_attn_w_kv_down", "L0_attn_w_kv_up", "L0_attn_w_q", "L0_attn_w_out", "L0_ffn_rW",
        "L0_ffn_rb", "L0_ffn_W1", "L0_ffn_b1", "L0_ffn_W2", "L0_ffn_b2", "L0_ffn_sW1", "L0_ffn_sb1",
        "L0_ffn_sW2", "L0_ffn_sb2"]


def kernel(**inputs):
    import concourse.bacc as _bacc
    from concourse.bass_utils import run_bass_kernel_spmd as _run

    nc = _bacc.Bacc("TRN2", target_bir_lowering=False, num_devices=1)
    arrays, args = {}, []
    for name in _INS:
        a = np.ascontiguousarray(inputs[name])
        arrays[f"in_{name}"] = a
        args.append(nc.dram_tensor(f"in_{name}", a.shape, mybir.dt.from_np(a.dtype), kind="ExternalInput").ap())
    shape = inputs["L0_attn_x"].shape
    args.append(nc.dram_tensor("out_x", shape, F32, kind="ExternalOutput").ap())
    macaron_kernel(nc, *args)
    r = _run(nc, [arrays], core_ids=[0])
    return r.results[0]["out_x"]
```
